# Optimizing a Trainium2 kernel written in Bass

```python
import numpy as np
import jax
import jax.numpy as jnp

def _softmax(x, axis=-1):
    return jax.nn.softmax(x, axis=axis)

def _gelu(x):
    return jax.nn.gelu(x, approximate=True)

def _silu(x):
    return jax.nn.silu(x)

def _sigmoid(x):
    return jax.nn.sigmoid(x)

def _layernorm(x, axis=-1, eps=1e-05):
    m = jnp.mean(x, axis=axis, keepdims=True)
    v = jnp.var(x, axis=axis, keepdims=True)
    return (x - m) / jnp.sqrt(v + eps)

def _scatter_add(tgt, idx, src, axis=0):
    return tgt.at[idx].add(src)

def _segment_sum(src, seg, n):
    return jax.ops.segment_sum(src, seg, n)
kernel_name = 'mk_seq_postln_d1_jaxref_r4_e3a5a5'

def setup_inputs(seed: int=0):
    np.random.seed(seed)
    _w = jnp.asarray

    def _L0_attn_setup():
        import jax, jax.numpy as jnp
        import numpy as np
        import math
        HIDDEN = 1024
        N_HEADS = 32
        N_KV_HEADS = 8
        HEAD_DIM = HIDDEN // N_HEADS
        GROUPS = N_HEADS // N_KV_HEADS
        ROPE_THETA = 10000.0
        TOKEN_BUDGET = 128
        INIT_BUDGET = 128
        RECENT_BUDGET = 128
        CHUNK = 16
        B, S = (1, 512)

        def _rotate_half(x):
            x1, x2 = jnp.split(x, 2, axis=-1)
            return jnp.concatenate([-x2, x1], axis=-1)

        def _rope(seq_len, dtype):
            inv_freq = 1.0 / ROPE_THETA ** (jnp.arange(0, HEAD_DIM, 2, dtype=jnp.float32) / HEAD_DIM)
            freqs = jnp.arange(seq_len, dtype=jnp.float32)[:, None] * inv_freq[None, :]
            emb = jnp.concatenate([freqs, freqs], axis=-1)
            return (jnp.cos(emb).astype(dtype), jnp.sin(emb).astype(dtype))
        key = jax.random.key(seed)
        ks = jax.random.split(key, 5)
        sc = 0.02
        return {'hidden_states': jax.random.normal(ks[0], (B, S, HIDDEN), dtype=jnp.float32), 'wq': jax.random.normal(ks[1], (N_HEADS * HEAD_DIM, HIDDEN), dtype=jnp.float32) * sc, 'wk': jax.random.normal(ks[2], (N_KV_HEADS * HEAD_DIM, HIDDEN), dtype=jnp.float32) * sc, 'wv': jax.random.normal(ks[3], (N_KV_HEADS * HEAD_DIM, HIDDEN), dtype=jnp.float32) * sc, 'wo': jax.random.normal(ks[4], (HIDDEN, N_HEADS * HEAD_DIM), dtype=jnp.float32) * sc}
    _L0_attn_in = _L0_attn_setup()

    def _L0_ffn_setup():
        import jax, jax.numpy as jnp
        import numpy as np
        GROUP_SIZE = 128

        def dequantize(imatrix, scales, zeros, group_size, out_dtype):
            rs = jnp.repeat(scales, group_size, axis=0)
            rz = jnp.repeat(zeros, group_size, axis=0)
            return ((imatrix.astype(rs.dtype) - rz.astype(rs.dtype)) * rs).astype(out_dtype)
        key = jax.random.key(seed)
        ks = jax.random.split(key, 10)
        H, I, G = (1024, 3584, GROUP_SIZE)
        B, S = (4, 512)
        x = jax.random.normal(ks[0], (B, S, H), dtype=jnp.float32)
        gate_w = jax.random.randint(ks[1], (H, I), 0, 16, dtype=jnp.int32)
        gate_z = jax.random.randint(ks[2], (H // G, I), 0, 16, dtype=jnp.int32)
        gate_s = jax.random.uniform(ks[3], (H // G, I), dtype=jnp.float32) * 0.01
        up_w = jax.random.randint(ks[4], (H, I), 0, 16, dtype=jnp.int32)
        up_z = jax.random.randint(ks[5], (H // G, I), 0, 16, dtype=jnp.int32)
        up_s = jax.random.uniform(ks[6], (H // G, I), dtype=jnp.float32) * 0.01
        down_w = jax.random.randint(ks[7], (I, H), 0, 16, dtype=jnp.int32)
        down_z = jax.random.randint(ks[8], (I // G, H), 0, 16, dtype=jnp.int32)
        down_s = jax.random.uniform(ks[9], (I // G, H), dtype=jnp.float32) * 0.01
        return {'x': x, 'gate_w': gate_w, 'gate_z': gate_z, 'gate_s': gate_s, 'up_w': up_w, 'up_z': up_z, 'up_s': up_s, 'down_w': down_w, 'down_z': down_z, 'down_s': down_s}
    _L0_ffn_in = _L0_ffn_setup()
    _d = {'L0_attn_hidden_states': _L0_attn_in['hidden_states'], 'L0_attn_wq': _L0_attn_in['wq'], 'L0_attn_wk': _L0_attn_in['wk'], 'L0_attn_wv': _L0_attn_in['wv'], 'L0_attn_wo': _L0_attn_in['wo'], 'L0_ffn_gate_w': _L0_ffn_in['gate_w'], 'L0_ffn_gate_z': _L0_ffn_in['gate_z'], 'L0_ffn_gate_s': _L0_ffn_in['gate_s'], 'L0_ffn_up_w': _L0_ffn_in['up_w'], 'L0_ffn_up_z': _L0_ffn_in['up_z'], 'L0_ffn_up_s': _L0_ffn_in['up_s'], 'L0_ffn_down_w': _L0_ffn_in['down_w'], 'L0_ffn_down_z': _L0_ffn_in['down_z'], 'L0_ffn_down_s': _L0_ffn_in['down_s']}
    _x0 = _d['L0_attn_hidden_states']
    _d['L0_attn_hidden_states'] = jax.random.normal(jax.random.fold_in(jax.random.key(seed), 1), (4, 512, 1024), dtype=_x0.dtype)
    del _x0
    return _d

def reference(L0_attn_hidden_states, L0_attn_wq, L0_attn_wk, L0_attn_wv, L0_attn_wo, L0_ffn_gate_w, L0_ffn_gate_z, L0_ffn_gate_s, L0_ffn_up_w, L0_ffn_up_z, L0_ffn_up_s, L0_ffn_down_w, L0_ffn_down_z, L0_ffn_down_s):

    def _L0_attn_ref(hidden_states, wq, wk, wv, wo):
        import jax, jax.numpy as jnp
        import numpy as np
        import math
        HIDDEN = 1024
        N_HEADS = 32
        N_KV_HEADS = 8
        HEAD_DIM = HIDDEN // N_HEADS
        GROUPS = N_HEADS // N_KV_HEADS
        ROPE_THETA = 10000.0
        TOKEN_BUDGET = 128
        INIT_BUDGET = 128
        RECENT_BUDGET = 128
        CHUNK = 16
        B, S = (1, 512)

        def _rotate_half(x):
            x1, x2 = jnp.split(x, 2, axis=-1)
            return jnp.concatenate([-x2, x1], axis=-1)

        def _rope(seq_len, dtype):
            inv_freq = 1.0 / ROPE_THETA ** (jnp.arange(0, HEAD_DIM, 2, dtype=jnp.float32) / HEAD_DIM)
            freqs = jnp.arange(seq_len, dtype=jnp.float32)[:, None] * inv_freq[None, :]
            emb = jnp.concatenate([freqs, freqs], axis=-1)
            return (jnp.cos(emb).astype(dtype), jnp.sin(emb).astype(dtype))
        b, s, _ = hidden_states.shape
        dtype = hidden_states.dtype
        NEG = jnp.finfo(dtype).min
        q = (hidden_states @ wq.T).reshape(b, s, N_HEADS, HEAD_DIM).transpose(0, 2, 1, 3)
        k = (hidden_states @ wk.T).reshape(b, s, N_KV_HEADS, HEAD_DIM).transpose(0, 2, 1, 3)
        v = (hidden_states @ wv.T).reshape(b, s, N_KV_HEADS, HEAD_DIM).transpose(0, 2, 1, 3)
        cos, sin = _rope(s, dtype)
        q = q * cos[None, None] + _rotate_half(q) * sin[None, None]
        k = k * cos[None, None] + _rotate_half(k) * sin[None, None]
        k = jnp.repeat(k, GROUPS, axis=1)
        v = jnp.repeat(v, GROUPS, axis=1)
        scores = jnp.einsum('bhqd,bhkd->bhqk', q, k) / math.sqrt(HEAD_DIM)
        q_pos = jnp.arange(s)[:, None]
        k_pos = jnp.arange(s)[None, :]
        causal = k_pos <= q_pos
        masked = jnp.where(causal[None, None], scores, NEG)
        pad = -s % CHUNK
        padded = jnp.pad(masked, ((0, 0), (0, 0), (0, 0), (0, pad)), constant_values=NEG)
        n_chunks = (s + pad) // CHUNK
        chunk_max = padded.reshape(b, N_HEADS, s, n_chunks, CHUNK).max(axis=-1)
        k_top = min(max(3, TOKEN_BUDGET // CHUNK), n_chunks)
        _, topk_idx = jax.lax.top_k(chunk_max, k_top)
        chunk_mask = jnp.any(topk_idx[..., None] == jnp.arange(n_chunks), axis=-2)
        tok_mask = jnp.repeat(chunk_mask, CHUNK, axis=-1)[..., :s]
        init_mask = k_pos < INIT_BUDGET
        recent_mask = k_pos > q_pos - RECENT_BUDGET
        allowed = causal[None, None] & (tok_mask | init_mask[None, None] | recent_mask[None, None])
        final = jnp.where(allowed, scores, NEG)
        attn = jax.nn.softmax(final, axis=-1)
        out = jnp.einsum('bhqk,bhkd->bhqd', attn, v)
        out = out.transpose(0, 2, 1, 3).reshape(b, s, N_HEADS * HEAD_DIM)
        return out @ wo.T

    def _L0_ffn_ref(x, gate_w, gate_z, gate_s, up_w, up_z, up_s, down_w, down_z, down_s):
        import jax, jax.numpy as jnp
        import numpy as np
        GROUP_SIZE = 128

        def dequantize(imatrix, scales, zeros, group_size, out_dtype):
            rs = jnp.repeat(scales, group_size, axis=0)
            rz = jnp.repeat(zeros, group_size, axis=0)
            return ((imatrix.astype(rs.dtype) - rz.astype(rs.dtype)) * rs).astype(out_dtype)
        dt = x.dtype
        gate_proj = dequantize(gate_w, gate_s, gate_z, GROUP_SIZE, dt)
        up_proj = dequantize(up_w, up_s, up_z, GROUP_SIZE, dt)
        down_proj = dequantize(down_w, down_s, down_z, GROUP_SIZE, dt)
        gate = jax.nn.silu(jnp.dot(x, gate_proj))
        up = jnp.dot(x, up_proj)
        return jnp.dot(gate * up, down_proj)
    x = L0_attn_hidden_states
    x = _layernorm(x + _L0_attn_ref(x, L0_attn_wq, L0_attn_wk, L0_attn_wv, L0_attn_wo), axis=-1)
    x = _layernorm(x + _L0_ffn_ref(x, L0_ffn_gate_w, L0_ffn_gate_z, L0_ffn_gate_s, L0_ffn_up_w, L0_ffn_up_z, L0_ffn_up_s, L0_ffn_down_w, L0_ffn_down_z, L0_ffn_down_s), axis=-1)
    return x

_drawn_inputs = setup_inputs


def setup_inputs(seed=0):
    import zlib

    import numpy as np

    out = dict(_drawn_inputs(seed))
    spreads = {}
    factors = {}
    for name, (base, spread) in spreads.items():
        noise = np.random.default_rng([zlib.crc32(name.encode()), seed]).standard_normal(out[name].shape)
        drawn = base * np.exp(spread * noise) if base else spread * noise
        out[name] = jnp.asarray(drawn.astype(out[name].dtype))
    for name, factor in factors.items():
        out[name] = (out[name] * factor).astype(out[name].dtype)
    return out
```

```python
from contextlib import ExitStack

import numpy as np

import concourse.bass as bass
from concourse import mybir

F32 = mybir.dt.float32
F16 = mybir.dt.float16
I32 = mybir.dt.int32
ALU = mybir.AluOpType
ACT = mybir.ActivationFunctionType
AX = mybir.AxisListType

P = 128
BATCH, SEQ, HID = 4, 512, 1024
TOK = BATCH * SEQ
HEADS, KV_HEADS = 32, 8
HD = HID // HEADS
PER_KV = HEADS // KV_HEADS
KV = KV_HEADS * HD
QKV = HID + 2 * KV
KT = HID // P
SEQ_TILES = SEQ // P
CHUNK = 16
BLOCK_CHUNKS = P // CHUNK
N_CHUNKS = SEQ // CHUNK
TOP = 8
INNER = 3584
IC = 256
MLP_CHUNKS = INNER // IC
UNITS = 12
UW = 512
EPS = 1e-5
W_SCALE = 256.0
X1_SCALE = 16.0
MASKED = -30000.0
TAKEN = 3.0e38
TAKEN_OVER = 1.0e38
PARTS = ((0, 0), (0, 1), (1, 0))

X_CREDIT = 4
PROJ_CREDIT = 9
S_CREDIT = 2
ST_CREDIT = 37
EXP_CREDIT = 2
ONE = 1
STAGE_DMAS = 12
STAGE_COUNT = 16 * STAGE_DMAS


def hold(eng, passed):
    eng.sem_inc(passed, 1)


def host_constants():
    inv = (np.float32(1.0) / np.float32(10000.0) ** (np.arange(0, HD, 2, dtype=np.float32) / np.float32(HD))).astype(np.float32)
    freq = np.arange(SEQ, dtype=np.float32)[:, None] * inv[None, :]
    both = np.concatenate([freq, freq], axis=1).T
    sign = np.where(np.arange(HD) < HD // 2, -1.0, 1.0)[:, None].astype(np.float32)
    unscale = np.float32(1.0 / W_SCALE)
    cos = np.tile(np.cos(both) * unscale, (PER_KV, 1))
    sin = np.tile(np.sin(both) * sign * unscale, (PER_KV, 1))
    rotary = np.stack([cos, sin], axis=1).astype(np.float32)

    r = np.arange(P)
    c16 = np.zeros((P, 4 * P + SEQ), np.float16)
    c16[:, 0:P] = np.eye(P)
    c16[:, P:2 * P] = np.where(r[None, :] > r[:, None], MASKED, 0)
    c16[:, 2 * P:3 * P] = np.where(r[:, None] > r[None, :], MASKED, 0)
    c16[:, 3 * P:4 * P] = (r[:, None] // CHUNK == r[None, :] // CHUNK) & (r[None, :] <= r[:, None])
    c16[96:128, 4 * P:] = np.arange(SEQ)[None, :] // CHUNK == np.arange(N_CHUNKS)[:, None]

    c32 = np.zeros((P, 3 * N_CHUNKS), np.float32)
    qc = r // CHUNK
    for i in (2, 3):
        for c in range(BLOCK_CHUNKS, BLOCK_CHUNKS * i):
            block, cl = divmod(c, BLOCK_CHUNKS)
            full = np.ones(P, bool) if block < i - 1 else cl < qc
            c32[:, (i - 2) * N_CHUNKS + c] = np.where(full, MASKED, 0)
    for cl in range(BLOCK_CHUNKS):
        c32[:, 2 * N_CHUNKS + cl] = np.where(cl == qc, MASKED, 0)
    return rotary, c16, c32


def attention(nc, xT, x, wqkvT, woT, rotary, const16, const32, x1):
    with ExitStack() as ctx:
        sb = lambda name, shape, dt: ctx.enter_context(nc.sbuf_tensor(name, shape, dt))
        sem = lambda name: ctx.enter_context(nc.semaphore(name))

        wqkv = [sb(f"wqkv{p}", [P, KT, QKV], F16) for p in range(2)]
        wo = [sb(f"wo{p}", [P, KT, HID], F16) for p in range(2)]
        xs = [sb(f"xs{p}", [P, KT, SEQ], F16) for p in range(2)]
        xin = sb("xin", [P, 4, SEQ], F32)
        q_stack = sb("q_stack", [P, 4, PER_KV, SEQ], F16)
        k_stack = sb("k_stack", [P, KV_HEADS, SEQ], F16)
        stage = sb("stage", [P, 2, 2, SEQ], F16)
        probs = sb("probs", [P, PER_KV, 1280], F32)
        w_in = probs[:, :, :].rearrange("p a b -> p (a b)")
        ot = [sb(f"ot{p}", [P, KV_HEADS, SEQ], F16) for p in range(2)]
        v = sb("v", [P, SEQ_TILES, KV], F32)
        rot = sb("rot", [P, 2, SEQ], F32)
        c16 = sb("c16", [P, 4 * P + SEQ], F16)
        c32 = sb("c32", [P, 3 * N_CHUNKS], F32)
        ones = sb("ones", [P, HD], F32)
        zero = sb("zero", [P, N_CHUNKS], F32)
        r_cos = sb("r_cos", [P, SEQ], F32)
        r_sin = sb("r_sin", [P, SEQ], F32)
        r_out = sb("r_out", [P, SEQ], F32)
        row_inv = sb("row_inv", [P, SEQ], F32)
        o_norm = sb("o_norm", [P, SEQ], F32)
        chunk_max = sb("chunk_max", [P, 2, PER_KV, N_CHUNKS], F32)
        left = sb("left", [P, 2, PER_KV, N_CHUNKS], F32)
        top8 = sb("top8", [P, 2, PER_KV, TOP], F32)
        pen = sb("pen", [P, 2, PER_KV, N_CHUNKS], F32)
        pen_edge = sb("pen_edge", [P, 2, PER_KV, BLOCK_CHUNKS], F32)
        edge = sb("edge", [P, 2, PER_KV], F32)
        bias = sb("bias", [P, SEQ_TILES, PER_KV, N_CHUNKS], F16)
        edge_diag = sb("edge_diag", [P, 2, PER_KV, P], F16)
        y = sb("y", [P, 2, HID], F32)
        stats = sb("stats", [P, 2, 2, 6], F32)
        mean_var = sb("mean_var", [P, 2, 2], F32)
        var_eps = sb("var_eps", [P, 2], F32)
        rstd = sb("rstd", [P, 2], F32)
        power = sb("power", [P, 1], F32)

        bank = [ctx.enter_context(nc.psum_tensor(f"bank{i}", [P, 512], F32)) for i in range(8)]
        s_bank, st_bank, proj_bank = bank[0:2], bank[2:4], bank[4:6]
        o_bank, sum_bank = bank[6], bank[7]
        bias_t = [st_bank[k][:, :].bitcast(F16) for k in range(2)]

        ident = c16[:, 0:P]
        causal_qk = c16[:, P:2 * P]
        causal_kq = c16[:, 2 * P:3 * P]
        same_chunk = c16[:, 3 * P:4 * P]

        const_in = sem("const_in")
        indicator_in = sem("indicator_in")
        w_loaded = [sem(f"w_loaded{s}") for s in range(2)]
        w_hi = sem("w_hi")
        w_lo = sem("w_lo")
        x_loaded = [sem(f"x_loaded{s}") for s in range(4)]
        x_hi = sem("x_hi")
        x_lo = sem("x_lo")
        proj_done = sem("proj_done")
        proj_read = sem("proj_read")
        rotated = sem("rotated")
        rot_hi = sem("rot_hi")
        stage_full = sem("stage_full")
        stage_sent = [sem(f"stage_sent{s}") for s in range(2)]
        s_done = sem("s_done")
        s_read = sem("s_read")
        bias_done = sem("bias_done")
        edge_done = sem("edge_done")
        bias_turned = sem("bias_turned")
        bias_in_a = sem("bias_in_a")
        bias_in_d = sem("bias_in_d")
        st_done = sem("st_done")
        exp_done = sem("exp_done")
        pv_done = sem("pv_done")
        o_read = sem("o_read")
        ot_done = sem("ot_done")
        y_loaded = [sem(f"y_loaded{s}") for s in range(2)]
        y_stored = [sem(f"y_stored{s}") for s in range(2)]
        y_done = sem("y_done")
        var_done = sem("var_done")
        rstd_done = sem("rstd_done")
        pool_set = sem("pool_set")
        dve_step = sem("dve_step")
        passed = sem("passed")

        K0, V0, Q0, Y0, PROJ = 0, 2, 6, 14, 22
        GROUP_S = PER_KV * SEQ_TILES
        PIECES = (((0, 0),), ((0, 1), (384, 3)), ((0, 2),))
        PIECE_AT, PIECE_N = (0, 512, 1024), (512, 512, 256)
        KEY_AT = (0, 512, 1024, 512 + 384)
        GROUP_ST = PER_KV * len(PIECES)

        block = ctx.enter_context(nc.Block())

        @block.sync
        def _(sp):
            sp.dma_start(c16[:, :], const16).then_inc(const_in, 16)
            sp.dma_start(c32[:, :], const32).then_inc(const_in, 16)
            sp.dma_start(rot[:, :, :], rotary).then_inc(const_in, 16)
            for kv in range(KV_HEADS):
                sp.dma_start(k_stack[96:128, kv, :], const16[96:128, 4 * P:]).then_inc(indicator_in, 16)
            for u in range(2 * KT):
                if u >= 2:
                    sp.wait_ge(w_lo, u - 1)
                kt, s = u % KT, u % 2
                if u < KT:
                    dst, src = w_in[:, s * QKV:(s + 1) * QKV], wqkvT[kt * P:(kt + 1) * P, :]
                else:
                    dst, src = w_in[:, 2 * QKV + s * HID:2 * QKV + (s + 1) * HID], woT[kt * P:(kt + 1) * P, :]
                sp.dma_start(dst, src).then_inc(w_loaded[s], 16)
            with sp.Fori(0, BATCH) as b:
                for kt in range(KT):
                    sp.wait_ge(x_lo, b * KT + kt + 1)
                    hold(sp, passed)
                    sp.dma_start(xin[:, kt % 4, :], xT[b, kt * P:(kt + 1) * P, :]).then_inc(x_loaded[kt % 4], 16)
                for n in range(2 + KV_HEADS):
                    s = n % 2
                    sp.wait_ge(stage_full, b * 10 + n + 1)
                    hold(sp, passed)
                    if n == 0:
                        sp.wait_ge(st_done, b * (KV_HEADS * GROUP_ST) + ST_CREDIT)
                    if n >= 2:
                        sp.wait_ge(st_done, b * (KV_HEADS * GROUP_ST) + (n - 2 - 3) * GROUP_ST + ST_CREDIT)
                    for j in range(PER_KV):
                        for row, part in enumerate((0, 0, 1) if n < 2 else (0, 1, 0)):
                            to = (k_stack[32 * row:32 * row + 32, PER_KV * n + j, :] if n < 2 else
                                  q_stack[32 * row:32 * row + 32, (n - 2) % 4, j, :])
                            sp.dma_start(to, stage[32 * j:32 * j + 32, s, part, :]).then_inc(stage_sent[s], 16)
                for t in range(SEQ_TILES):
                    s = t % 2
                    if t < 2:
                        sp.wait_ge(y_stored[s], b * 32 + 16)
                        hold(sp, passed)
                        sp.dma_start(y[:, s, :], x[b, t * P:(t + 1) * P, :]).then_inc(y_loaded[s], 16)
                for t in range(SEQ_TILES):
                    s = t % 2
                    sp.wait_ge(y_done, b * SEQ_TILES + t + 1)
                    hold(sp, passed)
                    sp.dma_start(x1[b, t * P:(t + 1) * P, :], y[:, s, :]).then_inc(y_stored[s], 16)
                    if t + 2 < SEQ_TILES:
                        sp.wait_ge(y_stored[s], b * 32 + 32)
                        hold(sp, passed)
                        sp.dma_start(y[:, s, :], x[b, (t + 2) * P:(t + 3) * P, :]).then_inc(y_loaded[s], 16)
            for s in range(2):
                sp.wait_ge(y_stored[s], 16 + BATCH * 32)

        @block.gpsimd
        def _(pool):
            pool.sem_inc(st_done, ST_CREDIT)
            pool.sem_inc(proj_done, PROJ_CREDIT)
            pool.sem_inc(bias_turned, ONE)
            pool.sem_inc(pv_done, ONE)
            for s in range(2):
                pool.sem_inc(stage_sent[s], STAGE_COUNT)
                pool.sem_inc(y_stored[s], 16)
            nc.gpsimd.memset(power[:, :], -0.5).then_inc(pool_set, 1)
            nc.gpsimd.memset(ones[:, :], 1.0).then_inc(pool_set, 1)
            nc.gpsimd.memset(zero[:, :], 0.0).then_inc(pool_set, 1)
            nc.gpsimd.memset(bias[:, :, :, :], 0.0).then_inc(pool_set, 1)
            pool.wait_ge(pool_set, 4)
            with pool.Fori(0, BATCH) as b:
                for t in range(SEQ_TILES):
                    s = t % 2
                    pool.wait_ge(var_done, b * SEQ_TILES + t + 1)
                    nc.gpsimd.tensor_tensor(rstd[:, s:s + 1], var_eps[:, s:s + 1], power[:, :], ALU.pow).then_inc(rstd_done, 1)

        @block.scalar
        def _(act):
            for u in range(2 * KT):
                kt, s = u % KT, u % 2
                act.wait_ge(w_loaded[s], 16 * (u // 2 + 1))
                if u < KT:
                    nc.scalar.activation(wqkv[0][:, kt, :], w_in[:, s * QKV:(s + 1) * QKV], ACT.Copy, scale=W_SCALE).then_inc(w_hi, 1)
                else:
                    nc.scalar.activation(wo[0][:, kt, :], w_in[:, 2 * QKV + s * HID:2 * QKV + (s + 1) * HID], ACT.Copy,
                                         scale=W_SCALE).then_inc(w_hi, 1)
            act.sem_inc(exp_done, EXP_CREDIT)

            with act.Fori(0, BATCH) as b:
                def rotated_hi(n):
                    act.wait_ge(rotated, b * 10 + n + 1)
                    act.wait_ge(stage_sent[n % 2], b * (5 * STAGE_COUNT) + (n // 2 + 1) * STAGE_COUNT)
                    nc.scalar.activation(stage[:, n % 2, 0, :], r_out[:, :], ACT.Copy).then_inc(rot_hi, 1)

                act.wait_ge(proj_done, b * PROJ + 1)
                for kt in range(KT):
                    act.wait_ge(x_loaded[kt % 4], b * 32 + 16 * (kt // 4 + 1))
                    nc.scalar.activation(xs[0][:, kt, :], xin[:, kt % 4, :], ACT.Copy).then_inc(x_hi, 1)
                for n in range(4):
                    rotated_hi(n)
                for g in range(KV_HEADS):
                    if g + 2 < KV_HEADS:
                        rotated_hi(g + 4)
                    slot = g % 4
                    act.wait_ge(bias_turned, b * (2 * KV_HEADS) + 2 * g + 1 + ONE)
                    nc.scalar.activation(q_stack[96:128, slot, 0:2, :], bias_t[0][96:128, :].rearrange("p (j n) -> p j n", j=2),
                                         ACT.Copy).then_inc(bias_in_a, 1)
                    act.wait_ge(pv_done, b * KV_HEADS + g + ONE)
                    for j in range(PER_KV):
                        for k in range(len(PIECES)):
                            u = j * len(PIECES) + k
                            act.wait_ge(st_done, b * (KV_HEADS * GROUP_ST) + g * GROUP_ST + u + 1 + ST_CREDIT)
                            nc.scalar.activation(probs[:, j, PIECE_AT[k]:PIECE_AT[k] + PIECE_N[k]], st_bank[u % 2][:, 0:PIECE_N[k]],
                                                 ACT.Exp, scale=float(HD) ** -0.5).then_inc(exp_done, 1)

        @block.tensor
        def _(pe):
            def product(out, lhs, rhs, n):
                def one(i):
                    kt, (a, c) = i // 3, PARTS[i % 3]
                    return nc.tensor.matmul(out, lhs(a, kt), rhs(c, kt), start=(i == 0), stop=(i == 3 * KT - 1))
                return [lambda i=i: one(i) for i in range(n)]

            pe.wait_ge(const_in, 48)
            pe.wait_ge(indicator_in, 16 * KV_HEADS)
            pe.wait_ge(pool_set, 4)
            pe.wait_ge(w_lo, KT)
            with pe.Fori(0, BATCH) as b:
                def proj(p, passes):
                    pe.wait_ge(proj_read, b * PROJ + p + 1)
                    for f in passes[:-1]:
                        f()
                    passes[-1]().then_inc(proj_done, 1)

                def head_tile(p, c):
                    return product(proj_bank[p % 2][:, :], lambda a, kt: wqkv[a][:, kt, c * P:(c + 1) * P],
                                   lambda a, kt: xs[a][:, kt, :], 3 * KT)

                def scores(g, i, j):
                    u = i * PER_KV + j
                    pe.wait_ge(s_read, b * (KV_HEADS * GROUP_S) + g * GROUP_S + u + 1)
                    n = P * (i + 1)
                    nc.tensor.matmul(s_bank[u % 2][:, 0:n], q_stack[0:96, g % 4, j, P * i:n], k_stack[0:96, g, 0:n],
                                     start=True, stop=True, skip_group_check=True)
                    nc.tensor.matmul(s_bank[u % 2][:, n - P:n], ident, causal_qk, start=False, stop=True,
                                     skip_group_check=True).then_inc(s_done, 1)

                def values(g):
                    calls = []
                    for kb in range(SEQ_TILES):
                        for bank_, lhs in ((o_bank, v[:, kb, HD * g:HD * (g + 1)]), (sum_bank, ones[:, :])):
                            def one(kb=kb, bank_=bank_, lhs=lhs):
                                for j in range(PER_KV):
                                    last = nc.tensor.matmul(bank_[32 * j:32 * j + 32, P * kb:SEQ], lhs,
                                                            probs[:, j, KEY_AT[kb]:KEY_AT[kb] + SEQ - P * kb],
                                                            start=(kb == 0), stop=True, skip_group_check=True)
                                return last
                            calls.append(one)
                    return calls

                def begin_values(g):
                    pe.wait_ge(exp_done, b * (KV_HEADS * GROUP_ST) + (g + 1) * GROUP_ST + EXP_CREDIT)
                    pe.wait_ge(o_read, b * KV_HEADS + g + ONE)

                pe.wait_ge(x_lo, b * KT + KT + X_CREDIT)
                for n in range(2):
                    proj(K0 + n, head_tile(K0 + n, KT + n))
                for t in range(SEQ_TILES):
                    p = V0 + t
                    proj(p, product(proj_bank[p % 2][:, 0:KV], lambda a, kt, t=t: xs[a][:, kt, t * P:(t + 1) * P],
                                    lambda a, kt: wqkv[a][:, kt, HID + KV:QKV], 3 * KT))
                for n in range(2):
                    proj(Q0 + n, head_tile(Q0 + n, n))
                for g in range(KV_HEADS):
                    pe.wait_ge(stage_sent[g % 2], b * (5 * STAGE_COUNT) + ((2 + g) // 2 + 2) * STAGE_COUNT)
                    query = head_tile(Q0 + g + 2, g + 2) if g + 2 < KV_HEADS else []
                    value = values(g - 1) if g else []
                    for u in range(GROUP_S):
                        scores(g, u // PER_KV, u % PER_KV)
                        if query and u < 8:
                            if u == 0:
                                pe.wait_ge(proj_read, b * PROJ + Q0 + g + 2 + 1)
                            for f in query[3 * u:3 * u + 3]:
                                last = f()
                            if u == 7:
                                last.then_inc(proj_done, 1)
                        if value and u >= 8:
                            if u == 8:
                                begin_values(g - 1)
                            last = value[u - 8]()
                            if u == 15:
                                last.then_inc(pv_done, 1)
                    pe.wait_ge(bias_done, b * (KV_HEADS * SEQ_TILES) + SEQ_TILES * (g + 1))
                    pe.wait_ge(exp_done, b * (KV_HEADS * GROUP_ST) + g * GROUP_ST + EXP_CREDIT)
                    for k in range(2):
                        for jj in range(2):
                            for i in range(SEQ_TILES):
                                at = jj * SEQ + i * P
                                last = nc.tensor.transpose(bias_t[k][96:128, at:at + P], bias[:, i, 2 * k + jj, :], ident)
                        last.then_inc(bias_turned, 1)
                    pe.wait_ge(bias_in_a, b * KV_HEADS + g + 1)
                    pe.wait_ge(bias_in_d, b * KV_HEADS + g + 1)
                    pe.wait_ge(edge_done, b * (2 * KV_HEADS) + 2 * g + 2)
                    for j in range(PER_KV):
                        for k, piece in enumerate(PIECES):
                            u = j * len(PIECES) + k
                            pe.wait_ge(exp_done, b * (KV_HEADS * GROUP_ST) + g * GROUP_ST + u - 1 + EXP_CREDIT)
                            out = st_bank[u % 2]
                            for at, kb in piece:
                                nc.tensor.matmul(out[:, at:at + SEQ - P * kb], k_stack[:, g, P * kb:P * (kb + 1)],
                                                 q_stack[:, g % 4, j, P * kb:SEQ], start=(at == 0), stop=True, skip_group_check=True)
                                last = nc.tensor.matmul(out[:, at:at + P], ident, causal_kq, start=False,
                                                        stop=True, skip_group_check=True)
                                if kb in (1, 2):
                                    last = nc.tensor.matmul(out[:, at + P:at + 2 * P], same_chunk, edge_diag[:, kb - 1, j, :],
                                                            start=False, stop=True, skip_group_check=True)
                            last.then_inc(st_done, 1)
                begin_values(KV_HEADS - 1)
                for f in values(KV_HEADS - 1):
                    last = f()
                last.then_inc(pv_done, 1)
                pe.wait_ge(w_lo, 2 * KT)
                pe.wait_ge(ot_done, b * KV_HEADS + KV_HEADS)
                for t in range(SEQ_TILES):
                    for h in range(2):
                        p = Y0 + 2 * t + h
                        proj(p, product(proj_bank[p % 2][:, :], lambda a, kt, t=t: ot[a][:, kt, t * P:(t + 1) * P],
                                        lambda a, kt, h=h: wo[a][:, kt, h * 512:(h + 1) * 512], 3 * KT))

        @block.vector
        def _(dve):
            for u in range(2 * KT):
                kt, s = u % KT, u % 2
                w32 = w_in[:, s * QKV:(s + 1) * QKV] if u < KT else w_in[:, 2 * QKV + s * HID:2 * QKV + (s + 1) * HID]
                w16 = wqkv if u < KT else wo
                dve.wait_ge(w_hi, u + 1)
                nc.vector.scalar_tensor_tensor(out=w16[1][:, kt, :], in0=w32, scalar=W_SCALE, in1=w16[0][:, kt, :],
                                               op0=ALU.mult, op1=ALU.subtract).then_inc(w_lo, 1)
            dve.sem_inc(x_lo, X_CREDIT)
            dve.sem_inc(proj_read, 2)
            dve.sem_inc(s_read, S_CREDIT)
            dve.sem_inc(o_read, ONE)
            dve.wait_ge(const_in, 48)
            dve.wait_ge(pool_set, 4)

            with dve.Fori(0, BATCH) as b:
                steps = [0]

                def step(ins):
                    steps[0] += 1
                    ins.then_inc(dve_step, 1)

                def stepped():
                    dve.wait_ge(dve_step, b * DVE_STEPS + steps[0])

                def rotate(n, p):
                    tile = proj_bank[p % 2][:, :]
                    dve.wait_ge(proj_done, b * PROJ + p + 1 + PROJ_CREDIT)
                    step(nc.vector.tensor_tensor(r_cos[:, :], tile, rot[:, 0, :], ALU.mult))
                    nc.vector.stream_shuffle(out=r_sin[:, :], in_=tile, mask=[(i + HD // 2) % HD for i in range(HD)]).then_inc(proj_read, 1)
                    dve.wait_ge(proj_read, b * PROJ + p + 1 + 2)
                    step(nc.vector.tensor_tensor(r_sin[:, :], r_sin[:, :], rot[:, 1, :], ALU.mult))
                    stepped()
                    nc.vector.tensor_tensor(r_out[:, :], r_cos[:, :], r_sin[:, :], ALU.add).then_inc(rotated, 1)
                    dve.wait_ge(rot_hi, b * 10 + n + 1)
                    nc.vector.tensor_tensor(stage[:, n % 2, 1, :], r_out[:, :], stage[:, n % 2, 0, :], ALU.subtract).then_inc(stage_full, 1)

                def row_tile(g, i):
                    n = BLOCK_CHUNKS * (i + 1)
                    s = i % 2
                    cm = chunk_max[:, s, :, 0:n]
                    for j in range(PER_KV):
                        u = i * PER_KV + j
                        dve.wait_ge(s_done, b * (KV_HEADS * GROUP_S) + g * GROUP_S + u + 1)
                        nc.vector.tensor_reduce(chunk_max[:, s, j, 0:n], s_bank[u % 2][:, 0:n * CHUNK].rearrange("p (c k) -> p c k", k=CHUNK),
                                                AX.X, ALU.max).then_inc(s_read, 1)
                    dve.wait_ge(s_read, b * (KV_HEADS * GROUP_S) + g * GROUP_S + (i + 1) * PER_KV + S_CREDIT)
                    hold(dve, passed)
                    for j in range(PER_KV):
                        last = nc.vector.max(top8[:, s, j, :], chunk_max[:, s, j, 0:n])
                    step(last)
                    stepped()
                    row_max = top8[:, s, :, 0:1].broadcast_to([P, PER_KV, n])
                    source = zero[:, 0:n].unsqueeze(1).broadcast_to([P, PER_KV, n])
                    if i >= 2:
                        hold(dve, passed)
                        for j in range(PER_KV):
                            last = nc.vector.match_replace(left[:, s, j, 0:n], top8[:, s, j, :], chunk_max[:, s, j, 0:n], TAKEN)
                        step(last)
                        stepped()
                        far = c32[:, (i - 2) * N_CHUNKS:(i - 2) * N_CHUNKS + n].unsqueeze(1).broadcast_to([P, PER_KV, n])
                        own = c32[:, 2 * N_CHUNKS:2 * N_CHUNKS + BLOCK_CHUNKS].unsqueeze(1).broadcast_to([P, PER_KV, BLOCK_CHUNKS])
                        nc.vector.scalar_tensor_tensor(out=pen[:, s, :, 0:n], in0=left[:, s, :, 0:n], scalar=TAKEN_OVER, in1=far,
                                                       op0=ALU.is_lt, op1=ALU.mult)
                        step(nc.vector.scalar_tensor_tensor(out=pen_edge[:, s, :, :], in0=left[:, s, :, BLOCK_CHUNKS * (i - 1):BLOCK_CHUNKS * i],
                                                            scalar=TAKEN_OVER, in1=own, op0=ALU.is_lt, op1=ALU.mult))
                        stepped()
                        step(nc.vector.tensor_reduce(edge[:, s, :], pen_edge[:, s, :, :], AX.X, ALU.add))
                        source = pen[:, s, :, 0:n]
                    if i == 0:
                        dve.wait_ge(bias_turned, b * (2 * KV_HEADS) + 2 * g + ONE)
                    nc.vector.tensor_tensor(bias[:, i, :, 0:n], source, row_max, ALU.subtract).then_inc(bias_done, 1)
                    if i >= 2:
                        stepped()
                        if i == 2:
                            dve.wait_ge(st_done, b * (KV_HEADS * GROUP_ST) + g * GROUP_ST + ST_CREDIT)
                        for j in range(PER_KV):
                            last = nc.vector.tensor_scalar(edge_diag[:, i - 2, j, :], ident, edge[:, s, j:j + 1], None, ALU.mult)
                        last.then_inc(edge_done, 1)

                def normalise(g):
                    dve.wait_ge(pv_done, b * KV_HEADS + g + 1 + ONE)
                    step(nc.vector.reciprocal(row_inv[:, :], sum_bank[:, :]))
                    stepped()
                    nc.vector.tensor_tensor(o_norm[:, :], o_bank[:, :], row_inv[:, :], ALU.mult).then_inc(o_read, 1)
                    dve.wait_ge(o_read, b * KV_HEADS + g + 1 + ONE)
                    if g == 0:
                        dve.wait_ge(proj_done, b * PROJ + PROJ_CREDIT)
                    step(nc.vector.tensor_copy(ot[0][:, g, :], o_norm[:, :]))
                    stepped()
                    nc.vector.tensor_tensor(ot[1][:, g, :], o_norm[:, :], ot[0][:, g, :], ALU.subtract).then_inc(ot_done, 1)

                for kt in range(KT):
                    dve.wait_ge(x_hi, b * KT + kt + 1)
                    nc.vector.tensor_tensor(xs[1][:, kt, :], xin[:, kt % 4, :], xs[0][:, kt, :], ALU.subtract).then_inc(x_lo, 1)
                for n in range(2):
                    rotate(n, K0 + n)
                for t in range(SEQ_TILES):
                    p = V0 + t
                    dve.wait_ge(proj_done, b * PROJ + p + 1 + PROJ_CREDIT)
                    if t == 0:
                        dve.wait_ge(pv_done, b * KV_HEADS + ONE)
                    nc.vector.tensor_copy(v[:, t, :], proj_bank[p % 2][:, 0:KV]).then_inc(proj_read, 1)
                for n in range(2):
                    rotate(2 + n, Q0 + n)
                for g in range(KV_HEADS):
                    for i in range(SEQ_TILES):
                        row_tile(g, i)
                        if i == 2 and g + 2 < KV_HEADS:
                            rotate(g + 4, Q0 + g + 2)
                    dve.wait_ge(bias_turned, b * (2 * KV_HEADS) + 2 * g + 2 + ONE)
                    nc.vector.tensor_copy(q_stack[96:128, g % 4, 2:4, :], bias_t[1][96:128, :].rearrange("p (j n) -> p j n", j=2)).then_inc(bias_in_d, 1)
                    if g:
                        normalise(g - 1)
                normalise(KV_HEADS - 1)
                for t in range(SEQ_TILES):
                    s = t % 2
                    dve.wait_ge(y_loaded[s], b * 32 + 16 * (t // 2 + 1))
                    for h in range(2):
                        p = Y0 + 2 * t + h
                        half = y[:, s, h * 512:(h + 1) * 512]
                        dve.wait_ge(proj_done, b * PROJ + p + 1 + PROJ_CREDIT)
                        nc.vector.scalar_tensor_tensor(out=half, in0=proj_bank[p % 2][:, :], scalar=1.0 / (W_SCALE * W_SCALE), in1=half,
                                                       op0=ALU.mult, op1=ALU.add).then_inc(proj_read, 1)
                        dve.wait_ge(proj_read, b * PROJ + p + 1 + 2)
                        step(nc.vector.bn_stats(stats[:, s, h, :], half))
                    stepped()
                    hold(dve, passed)
                    step(nc.vector.bn_aggr(mean_var[:, s, :], stats[:, s, :, :].rearrange("p a b -> p (a b)")))
                    stepped()
                    nc.vector.tensor_scalar(var_eps[:, s:s + 1], mean_var[:, s, 1:2], EPS, None, ALU.add).then_inc(var_done, 1)
                    dve.wait_ge(rstd_done, b * SEQ_TILES + t + 1)
                    nc.vector.tensor_scalar(y[:, s, :], y[:, s, :], mean_var[:, s, 0:1], rstd[:, s:s + 1], ALU.subtract,
                                            ALU.mult).then_inc(y_done, 1)
                assert steps[0] == DVE_STEPS, steps


DVE_STEPS = 10 * 2 + KV_HEADS * (4 * 1 + 2 * 3) + KV_HEADS * 2 + SEQ_TILES * 3


def mlp(nc, x1, w_units, z_units, s_units, ident32, out):
    with ExitStack() as ctx:
        sb = lambda name, shape, dt: ctx.enter_context(nc.sbuf_tensor(name, shape, dt))
        sem = lambda name: ctx.enter_context(nc.semaphore(name))

        TILES = TOK // P
        TT = TOK // 512
        x1s = [sb(f"x1s{p}", [P, KT, TOK], F16) for p in range(2)]
        acc = sb("acc", [P, TILES, HID], F32)
        wset = [[sb(f"wset{s}{p}", [P, UNITS, UW], F16) for p in range(2)] for s in range(2)]
        w_raw = sb("w_raw", [P, 2, UW], I32)
        rows = sb("rows", [P, UW], F32)
        z_all = sb("z_all", [P, 2, UW], I32)
        s_all = sb("s_all", [P, 2, UW], F32)
        silu = sb("silu", [P, 2, 512], F32)
        hidden = sb("hidden", [P, 2, 512], F32)
        hs = [sb(f"hs{p}", [P, 2, 2, 512], F16) for p in range(2)]
        ident = hidden[:, 0, 0:P]
        stats = sb("stats2", [P, 4, 2, 6], F32)
        mean_var = sb("mean_var2", [P, 4, 2], F32)
        var_eps = sb("var_eps2", [P, 4], F32)
        rstd = sb("rstd2", [P, 4], F32)
        power = sb("power2", [P, 4], F32)
        bank = [ctx.enter_context(nc.psum_tensor(f"mbank{i}", [P, 512], F32)) for i in range(8)]
        gate_bank, up_bank, down_bank = bank[0:4:2], bank[1:4:2], bank[4:8]

        ident_in = sem("ident_in")
        acc_in = [sem(f"acc_in{k}") for k in range(TT)]
        turned = sem("turned")
        turned_hi = sem("turned_hi")
        turned_read = sem("turned_read")
        unit_in = [sem(f"unit_in{s}") for s in range(2)]
        spread = sem("spread")
        centred = sem("centred")
        scaled = sem("scaled")
        unit_hi = sem("unit_hi")
        unit_lo = sem("unit_lo")
        gu_done = sem("gu_done")
        silu_done = sem("silu_done")
        glu_done = sem("glu_done")
        h_hi = sem("h_hi")
        h_lo = sem("h_lo")
        down_done = sem("down_done")
        acc_done = sem("acc_done")
        stats_done = sem("stats_done")
        var_done = sem("var_done2")
        rstd_done = sem("rstd_done2")
        out_done = sem("out_done")
        stored = sem("stored")
        power_set = sem("power_set")
        passed = sem("passed2")

        DOWN_CREDIT = 33
        TILE_DOWNS = 8
        CHUNK_DOWNS = TT * TILE_DOWNS
        GLUS = 2 * TT
        PAIRS = MLP_CHUNKS // 2
        x1_rows = x1.rearrange("b (t p) h -> p (b t) h", p=P)
        out_rows = out.rearrange("b (t p) h -> p (b t) h", p=P)

        def pairs(eng, body):
            with eng.Fori(0, PAIRS - 1) as i:
                body(i * 2, 0, True)
                body(i * 2 + 1, 1, True)
            body(MLP_CHUNKS - 2, 0, True)
            body(MLP_CHUNKS - 1, 1, False)

        ORDER = (("glu", 0), ("glu", 1), ("down", 0), ("glu", 2), ("down", 1), ("glu", 3), ("down", 2), ("down", 3))
        BEHIND = {("glu", 0): (0, 1), ("glu", 1): (2, 3), ("down", 0): (4,), ("glu", 2): (5, 6), ("down", 1): (7,),
                  ("glu", 3): (8, 9), ("down", 2): (10,), ("down", 3): (11,)}

        block = ctx.enter_context(nc.Block())

        @block.sync
        def _(sp):
            def load_unit(c, k):
                s = k % 2
                sp.wait_ge(unit_lo, c * UNITS + k + 1)
                hold(sp, passed)
                sp.dma_start(w_raw[:, s, :], w_units[c, k]).then_inc(unit_in[s], 16)
                sp.dma_start(rows[64 * s:64 * s + 1, :], z_units[c, k:k + 1, :].bitcast(F32)).then_inc(unit_in[s], 16)
                sp.dma_start(rows[64 * s + 32:64 * s + 33, :], s_units[c, k:k + 1, :]).then_inc(unit_in[s], 16)

            sp.dma_start(ident, ident32).then_inc(ident_in, 16)
            for k in range(TT):
                sp.dma_start(acc[:, 4 * k:4 * k + 4, :], x1_rows[:, 4 * k:4 * k + 4, :]).then_inc(acc_in[k], 16)
            with sp.Fori(0, MLP_CHUNKS) as c:
                for k in range(UNITS):
                    load_unit(c, k)
            for t in range(TILES):
                sp.wait_ge(out_done, t + 1)
                sp.dma_start(out_rows[:, t, :], acc[:, t, :]).then_inc(stored, 16)
            sp.wait_ge(stored, 16 * TILES)

        @block.gpsimd
        def _(pool):
            pool.sem_inc(down_done, DOWN_CREDIT)
            nc.gpsimd.memset(power[:, :], -0.5).then_inc(power_set, 1)
            with pool.Fori(0, MLP_CHUNKS) as c:
                for k in range(UNITS):
                    s = k % 2
                    pool.wait_ge(unit_in[s], c * (48 * UNITS // 2) + 48 * (k // 2 + 1))
                    pool.wait_ge(scaled, c * UNITS + k + 1)
                    hold(pool, passed)
                    nc.gpsimd.partition_broadcast(z_all[:, s, :], rows[64 * s:64 * s + 1, :].bitcast(I32), channels=P).then_inc(spread, 1)
                    nc.gpsimd.partition_broadcast(s_all[:, s, :], rows[64 * s + 32:64 * s + 33, :], channels=P).then_inc(spread, 1)
            pool.wait_ge(power_set, 1)
            for k in range(TT):
                pool.wait_ge(var_done, k + 1)
                nc.gpsimd.tensor_tensor(rstd[:, :], var_eps[:, :], power[:, :], ALU.pow).then_inc(rstd_done, 1)

        @block.scalar
        def _(act):
            act.sem_inc(glu_done, 2)

            def unit_high(c, s, k):
                if k == 0:
                    act.wait_ge(down_done, c * CHUNK_DOWNS + 1)
                act.wait_ge(scaled, c * UNITS + k + 1 + 2)
                nc.scalar.activation(wset[s][0][:, k, :], w_raw[:, k % 2, :].bitcast(F32), ACT.Copy).then_inc(unit_hi, 1)

            for k in range(UNITS):
                unit_high(0, 0, k)
            for r in range(2 * TILES):
                t, h = divmod(r, 2)
                act.wait_ge(turned, r + 1)
                nc.scalar.activation(x1s[0][:, 4 * h:4 * h + 4, t * P:(t + 1) * P], down_bank[r % 4][:, :].rearrange("p (k t) -> p k t", k=4),
                                     ACT.Copy, scale=X1_SCALE).then_inc(turned_hi, 1)

            def chunk(c, s, more):
                for kind, tt in ORDER:
                    behind = BEHIND[kind, tt] if more else ()
                    if kind == "glu":
                        for j in range(2):
                            n = 2 * tt + j
                            act.wait_ge(gu_done, c * GLUS + n + 1)
                            act.wait_ge(glu_done, c * GLUS + n + 1)
                            nc.scalar.activation(silu[:, j, :], gate_bank[j][:, :], ACT.Silu, scale=1.0 / (W_SCALE * X1_SCALE)).then_inc(silu_done, 1)
                            act.wait_ge(glu_done, c * GLUS + n + 1 + 2)
                            act.wait_ge(down_done, c * CHUNK_DOWNS + TILE_DOWNS * (tt - 1) + DOWN_CREDIT)
                            nc.scalar.activation(hs[0][:, tt % 2, j, :], hidden[:, j, :], ACT.Copy).then_inc(h_hi, 1)
                            if behind:
                                unit_high(c + 1, 1 - s, behind[j])
                    elif behind:
                        unit_high(c + 1, 1 - s, behind[0])

            pairs(act, chunk)

        @block.tensor
        def _(pe):
            pe.wait_ge(ident_in, 16)
            for r in range(2 * TILES):
                t, h = divmod(r, 2)
                if r % 8 == 0:
                    pe.wait_ge(acc_in[r // 8], 16)
                if r >= 4:
                    pe.wait_ge(turned_read, r - 3)
                for k in range(4):
                    last = nc.tensor.transpose(down_bank[r % 4][:, k * P:(k + 1) * P], acc[:, t, (4 * h + k) * P:(4 * h + k + 1) * P], ident)
                last.then_inc(turned, 1)
            pe.wait_ge(turned_read, 2 * TILES)

            def chunk(c, s, more):
                for kind, tt in ORDER:
                    if kind == "glu":
                        for j in range(2):
                            n = 2 * tt + j
                            if n == 0:
                                pe.wait_ge(unit_lo, c * UNITS + 8 + 2)
                            pe.wait_ge(glu_done, c * GLUS + n + 1)
                            for first, to in ((0, gate_bank), (4, up_bank)):
                                for i in range(3 * KT):
                                    kt, (a, x) = i // 3, PARTS[i % 3]
                                    last = nc.tensor.matmul(to[j][:, :], wset[s][a][:, first + kt // 2, (kt % 2) * IC + j * P:(kt % 2) * IC + (j + 1) * P],
                                                            x1s[x][:, kt, 512 * tt:512 * (tt + 1)], start=(i == 0), stop=(i == 3 * KT - 1))
                            last.then_inc(gu_done, 1)
                    else:
                        if tt == 0:
                            pe.wait_ge(unit_lo, c * UNITS + UNITS + 2)
                        pe.wait_ge(h_lo, c * GLUS + 2 * tt + 2)
                        for m in range(TILE_DOWNS):
                            tl, h = divmod(m, 2)
                            pe.wait_ge(acc_done, c * CHUNK_DOWNS + TILE_DOWNS * tt + m + 1)
                            for i in range(6):
                                j, (a, w) = i // 3, PARTS[i % 3]
                                last = nc.tensor.matmul(down_bank[m % 4][:, :], hs[a][:, tt % 2, j, tl * P:(tl + 1) * P],
                                                        wset[s][w][:, 8 + 2 * j + h, :], start=(i == 0), stop=(i == 5))
                            last.then_inc(down_done, 1)

            pairs(pe, chunk)

        @block.vector
        def _(dve):
            dve.sem_inc(unit_lo, 2)
            dve.sem_inc(scaled, 2)
            dve.sem_inc(acc_done, 4)

            def unit_scale(c, k):
                s = k % 2
                raw, w = w_raw[:, s, :], w_raw[:, s, :].bitcast(F32)
                dve.wait_ge(spread, c * (2 * UNITS) + 2 * k + 2)
                dve.wait_ge(unit_in[s], c * (48 * UNITS // 2) + 48 * (k // 2 + 1))
                nc.vector.tensor_tensor(w, raw, z_all[:, s, :], ALU.subtract).then_inc(centred, 1)
                dve.wait_ge(centred, c * UNITS + k + 1)
                nc.vector.scalar_tensor_tensor(out=w, in0=w, scalar=W_SCALE, in1=s_all[:, s, :], op0=ALU.mult, op1=ALU.mult).then_inc(scaled, 1)

            def unit_low(c, s, k):
                dve.wait_ge(unit_hi, c * UNITS + k + 1)
                nc.vector.tensor_tensor(wset[s][1][:, k, :], w_raw[:, k % 2, :].bitcast(F32), wset[s][0][:, k, :], ALU.subtract).then_inc(unit_lo, 1)

            for k in range(UNITS):
                unit_scale(0, k)
                if k:
                    unit_low(0, 0, k - 1)
            unit_low(0, 0, UNITS - 1)
            for r in range(2 * TILES):
                t, h = divmod(r, 2)
                dve.wait_ge(turned_hi, r + 1)
                nc.vector.scalar_tensor_tensor(out=x1s[1][:, 4 * h:4 * h + 4, t * P:(t + 1) * P],
                                               in0=down_bank[r % 4][:, :].rearrange("p (k t) -> p k t", k=4), scalar=X1_SCALE,
                                               in1=x1s[0][:, 4 * h:4 * h + 4, t * P:(t + 1) * P], op0=ALU.mult,
                                               op1=ALU.subtract).then_inc(turned_read, 1)

            def chunk(c, s, more):
                for kind, tt in ORDER:
                    behind = BEHIND[kind, tt] if more else ()
                    if kind == "glu":
                        for j in range(2):
                            n = 2 * tt + j
                            dve.wait_ge(silu_done, c * GLUS + n + 1)
                            nc.vector.scalar_tensor_tensor(out=hidden[:, j, :], in0=up_bank[j][:, :], scalar=1.0 / (W_SCALE * X1_SCALE),
                                                           in1=silu[:, j, :], op0=ALU.mult, op1=ALU.mult).then_inc(glu_done, 1)
                            if behind:
                                unit_scale(c + 1, behind[j])
                            dve.wait_ge(h_hi, c * GLUS + n + 1)
                            nc.vector.tensor_tensor(hs[1][:, tt % 2, j, :], hidden[:, j, :], hs[0][:, tt % 2, j, :],
                                                    ALU.subtract).then_inc(h_lo, 1)
                            if behind:
                                unit_low(c + 1, 1 - s, behind[j])
                    else:
                        for m in range(TILE_DOWNS):
                            tl, h = divmod(m, 2)
                            part = acc[:, 4 * tt + tl, 512 * h:512 * (h + 1)]
                            dve.wait_ge(down_done, c * CHUNK_DOWNS + TILE_DOWNS * tt + m + 1 + DOWN_CREDIT)
                            nc.vector.scalar_tensor_tensor(out=part, in0=down_bank[m % 4][:, :], scalar=1.0 / W_SCALE, in1=part,
                                                           op0=ALU.mult, op1=ALU.add).then_inc(acc_done, 1)
                            if behind and m == 2:
                                unit_scale(c + 1, behind[0])
                            if behind and m == 5:
                                unit_low(c + 1, 1 - s, behind[0])
                        if not more:
                            norm(c, tt)

            def norm(c, tt):
                dve.wait_ge(acc_done, c * CHUNK_DOWNS + TILE_DOWNS * (tt + 1) + 4)
                for t in range(4):
                    for h in range(2):
                        nc.vector.bn_stats(stats[:, t, h, :], acc[:, 4 * tt + t, 512 * h:512 * (h + 1)]).then_inc(stats_done, 1)
                dve.wait_ge(stats_done, 16 * tt + 8)
                for t in range(4):
                    nc.vector.bn_aggr(mean_var[:, t, :], stats[:, t, :, :].rearrange("p a b -> p (a b)")).then_inc(stats_done, 2)
                dve.wait_ge(stats_done, 16 * tt + 16)
                nc.vector.tensor_scalar(var_eps[:, :], mean_var[:, :, 1], EPS, None, ALU.add).then_inc(var_done, 1)
                dve.wait_ge(rstd_done, tt + 1)
                for t in range(4):
                    nc.vector.tensor_scalar(acc[:, 4 * tt + t, :], acc[:, 4 * tt + t, :], mean_var[:, t, 0:1], rstd[:, t:t + 1],
                                            ALU.subtract, ALU.mult).then_inc(out_done, 1)

            pairs(dve, chunk)


_OUT = ((BATCH, SEQ, HID), "float32")


def kernel(**inputs):
    import concourse.bacc as _bacc
    from concourse.bass_utils import run_bass_kernel_spmd as _run

    arr = {k: np.asarray(a) for k, a in inputs.items()}
    x = arr["L0_attn_hidden_states"]
    wqkvT = np.concatenate([arr["L0_attn_wq"], arr["L0_attn_wk"], arr["L0_attn_wv"]], axis=0).T

    def wide(w):
        return w.reshape(4, 2, P, MLP_CHUNKS, IC).transpose(3, 0, 2, 1, 4).reshape(MLP_CHUNKS, 4, P, UW)

    def wide_rows(z):
        return z.reshape(4, 2, MLP_CHUNKS, IC).transpose(2, 0, 1, 3).reshape(MLP_CHUNKS, 4, UW)

    def tall(w):
        return w.reshape(MLP_CHUNKS, 2, P, 2, UW).transpose(0, 1, 3, 2, 4).reshape(MLP_CHUNKS, 4, P, UW)

    def tall_rows(z):
        return z.reshape(MLP_CHUNKS, 4, UW)

    g, u, d = "L0_ffn_gate_", "L0_ffn_up_", "L0_ffn_down_"
    rotary, const16, const32 = host_constants()
    arrays = {
        "x": x,
        "xT": x.transpose(0, 2, 1),
        "wqkvT": wqkvT,
        "woT": arr["L0_attn_wo"].T,
        "w_units": np.concatenate([wide(arr[g + "w"]), wide(arr[u + "w"]), tall(arr[d + "w"])], axis=1),
        "z_units": np.concatenate([wide_rows(arr[g + "z"]), wide_rows(arr[u + "z"]), tall_rows(arr[d + "z"])], axis=1),
        "s_units": np.concatenate([wide_rows(arr[g + "s"]), wide_rows(arr[u + "s"]), tall_rows(arr[d + "s"])], axis=1),
        "rotary": rotary,
        "const16": const16,
        "const32": const32,
        "ident32": np.eye(P, dtype=np.float32),
    }
    arrays = {k: np.ascontiguousarray(a) for k, a in arrays.items()}

    nc = _bacc.Bacc("TRN2", target_bir_lowering=False, num_devices=1)
    d_in = {k: nc.dram_tensor(k, a.shape, mybir.dt.from_np(a.dtype), kind="ExternalInput").ap() for k, a in arrays.items()}
    out = nc.dram_tensor("out", _OUT[0], F32, kind="ExternalOutput").ap()
    x1 = nc.dram_tensor("x1", _OUT[0], F32, kind="Internal").ap()
    attention(nc, d_in["xT"], d_in["x"], d_in["wqkvT"], d_in["woT"], d_in["rotary"], d_in["const16"], d_in["const32"], x1)
    mlp(nc, x1, d_in["w_units"], d_in["z_units"], d_in["s_units"], d_in["ident32"], out)
    r = _run(nc, [arrays], core_ids=[0])
    return r.results[0]["out"]
```

```python
from contextlib import ExitStack

import numpy as np

import concourse.bass as bass
from concourse import mybir

F32 = mybir.dt.float32
F16 = mybir.dt.float16
I32 = mybir.dt.int32
ALU = mybir.AluOpType
ACT = mybir.ActivationFunctionType
AX = mybir.AxisListType

P = 128
BATCH, SEQ, HID = 4, 512, 1024
TOK = BATCH * SEQ
HEADS, KV_HEADS = 32, 8
HD = HID // HEADS
PER_KV = HEADS // KV_HEADS
KV = KV_HEADS * HD
QKV = HID + 2 * KV
KT = HID // P
SEQ_TILES = SEQ // P
CHUNK = 16
BLOCK_CHUNKS = P // CHUNK
N_CHUNKS = SEQ // CHUNK
TOP = 8
INNER = 3584
IC = 256
MLP_CHUNKS = INNER // IC
UNITS = 12
UW = 512
EPS = 1e-5
W_SCALE = 256.0
X1_SCALE = 16.0
MASKED = -30000.0
TAKEN = 3.0e38
TAKEN_OVER = 1.0e38
PARTS = ((0, 0), (0, 1), (1, 0))

X_CREDIT = 4
PROJ_CREDIT = 9
PROJ_READ_CREDIT = 2
S_CREDIT = 3
ST_CREDIT = 37
EXP_CREDIT = 2
ONE = 1
EDGE_CREDIT = 2
W_SLOTS = 3
STAGE_DMAS = 12
STAGE_COUNT = 16 * STAGE_DMAS


def hold(eng, passed):
    eng.sem_inc(passed, 1)


def host_constants():
    inv = (np.float32(1.0) / np.float32(10000.0) ** (np.arange(0, HD, 2, dtype=np.float32) / np.float32(HD))).astype(np.float32)
    freq = np.arange(SEQ, dtype=np.float32)[:, None] * inv[None, :]
    both = np.concatenate([freq, freq], axis=1).T
    sign = np.where(np.arange(HD) < HD // 2, -1.0, 1.0)[:, None].astype(np.float32)
    unscale = np.float32(1.0 / W_SCALE)
    cos = np.tile(np.cos(both) * unscale, (PER_KV, 1))
    sin = np.tile(np.sin(both) * sign * unscale, (PER_KV, 1))
    rotary = np.stack([cos, sin], axis=1).astype(np.float32)

    r = np.arange(P)
    c16 = np.zeros((P, 4 * P + SEQ), np.float16)
    c16[:, 0:P] = np.eye(P)
    c16[:, P:2 * P] = np.where(r[None, :] > r[:, None], MASKED, 0)
    c16[:, 2 * P:3 * P] = np.where(r[:, None] > r[None, :], MASKED, 0)
    c16[:, 3 * P:4 * P] = (r[:, None] // CHUNK == r[None, :] // CHUNK) & (r[None, :] <= r[:, None])
    c16[96:128, 4 * P:] = np.arange(SEQ)[None, :] // CHUNK == np.arange(N_CHUNKS)[:, None]

    c32 = np.zeros((P, 3 * N_CHUNKS), np.float32)
    qc = r // CHUNK
    for i in (2, 3):
        for c in range(BLOCK_CHUNKS, BLOCK_CHUNKS * i):
            block, cl = divmod(c, BLOCK_CHUNKS)
            full = np.ones(P, bool) if block < i - 1 else cl < qc
            c32[:, (i - 2) * N_CHUNKS + c] = np.where(full, MASKED, 0)
    for cl in range(BLOCK_CHUNKS):
        c32[:, 2 * N_CHUNKS + cl] = np.where(cl == qc, MASKED, 0)
    return rotary, c16, c32


def attention(nc, xT, x, wqkvT, woT, rotary, const16, const32, x1):
    with ExitStack() as ctx:
        sb = lambda name, shape, dt: ctx.enter_context(nc.sbuf_tensor(name, shape, dt))
        sem = lambda name: ctx.enter_context(nc.semaphore(name))

        wqkv = [sb(f"wqkv{p}", [P, KT, QKV], F16) for p in range(2)]
        wo = [sb(f"wo{p}", [P, KT, HID], F16) for p in range(2)]
        xs = [sb(f"xs{p}", [P, KT, SEQ], F16) for p in range(2)]
        xin = sb("xin", [P, 4, SEQ], F32)
        q_stack = sb("q_stack", [P, 4, PER_KV, SEQ], F16)
        k_stack = sb("k_stack", [P, KV_HEADS, SEQ], F16)
        stage = sb("stage", [P, 2, 2, SEQ], F16)
        probs = sb("probs", [P, PER_KV, 1280], F32)
        w_in = probs[:, :, :].rearrange("p a b -> p (a b)")
        ot = [sb(f"ot{p}", [P, KV_HEADS, SEQ], F16) for p in range(2)]
        v = sb("v", [P, SEQ_TILES, KV], F32)
        rot = sb("rot", [P, 2, SEQ], F32)
        c16 = sb("c16", [P, 4 * P + SEQ], F16)
        c32 = sb("c32", [P, 3 * N_CHUNKS], F32)
        ones = sb("ones", [P, HD], F32)
        zero = sb("zero", [P, N_CHUNKS], F32)
        r_cos = sb("r_cos", [P, SEQ], F32)
        r_sin = sb("r_sin", [P, SEQ], F32)
        r_out = sb("r_out", [P, SEQ], F32)
        sum_turned = sb("sum_turned", [P, SEQ], F32)
        inv_turned = sb("inv_turned", [P, SEQ // 32], F32)
        row_inv = sb("row_inv", [P, SEQ], F32)
        o_norm = sb("o_norm", [P, SEQ], F32)
        chunk_max = sb("chunk_max", [P, 2, PER_KV, N_CHUNKS], F32)
        left = sb("left", [P, 2, PER_KV, N_CHUNKS], F32)
        top8 = sb("top8", [P, 2, PER_KV, TOP], F32)
        pen = sb("pen", [P, 2, PER_KV, N_CHUNKS], F32)
        pen_edge = sb("pen_edge", [P, 2, PER_KV, BLOCK_CHUNKS], F32)
        edge = sb("edge", [P, 2, PER_KV], F32)
        bias = sb("bias", [P, SEQ_TILES, PER_KV, N_CHUNKS], F16)
        edge_diag = sb("edge_diag", [P, 2, 2, PER_KV, P], F16)
        y = sb("y", [P, 2, HID], F32)
        stats = sb("stats", [P, 2, 2, 6], F32)
        mean_var = sb("mean_var", [P, 2, 2], F32)
        var_eps = sb("var_eps", [P, 2], F32)
        rstd = sb("rstd", [P, 2], F32)
        power = sb("power", [P, 1], F32)

        bank = [ctx.enter_context(nc.psum_tensor(f"bank{i}", [P, 512], F32)) for i in range(8)]
        s_bank, st_bank = bank[0:3], bank[3:5]
        o_bank, sum_bank = bank[6], bank[7]
        bias_t = [st_bank[k][:, :].bitcast(F16) for k in range(2)]

        ident = c16[:, 0:P]
        causal_qk = c16[:, P:2 * P]
        causal_kq = c16[:, 2 * P:3 * P]
        same_chunk = c16[:, 3 * P:4 * P]

        const_in = sem("const_in")
        indicator_in = sem("indicator_in")
        w_loaded = [sem(f"w_loaded{s}") for s in range(W_SLOTS)]
        w_hi = sem("w_hi")
        w_lo = sem("w_lo")
        x_loaded = [sem(f"x_loaded{s}") for s in range(4)]
        x_hi = sem("x_hi")
        x_lo = sem("x_lo")
        proj_done = sem("proj_done")
        proj_read = sem("proj_read")
        sin_done = sem("sin_done")
        rotated = sem("rotated")
        rot_hi = sem("rot_hi")
        o_done = sem("o_done")
        edge_ready = sem("edge_ready")
        stage_full = sem("stage_full")
        stage_sent = [sem(f"stage_sent{s}") for s in range(2)]
        s_done = sem("s_done")
        s_read = sem("s_read")
        bias_done = sem("bias_done")
        edge_done = sem("edge_done")
        bias_turned = sem("bias_turned")
        bias_in_a = sem("bias_in_a")
        bias_in_d = sem("bias_in_d")
        st_done = sem("st_done")
        exp_done = sem("exp_done")
        pv_done = sem("pv_done")
        o_read = sem("o_read")
        ot_done = sem("ot_done")
        y_loaded = [sem(f"y_loaded{s}") for s in range(2)]
        y_stored = [sem(f"y_stored{s}") for s in range(2)]
        y_done = sem("y_done")
        var_done = sem("var_done")
        rstd_done = sem("rstd_done")
        pool_set = sem("pool_set")
        dve_step = sem("dve_step")
        passed = sem("passed")

        def batches(eng, body):
            with eng.Fori(0, BATCH - 1) as b:
                body(b, True)
            body(BATCH - 1, False)

        K0, Q0, V0, Q1, Y0, PROJ = 0, 2, 3, 7, 14, 22

        def query_tile(n):
            return Q0 if n == 0 else Q1 + n - 1

        def proj_bank(p):
            return bank[5] if Q1 <= p < Y0 or p % 2 == 0 else s_bank[2]

        S_UNITS = [(0, range(4)), (1, range(2)), (1, range(2, 4))] + [(i, range(j, j + 1)) for i in (2, 3) for j in range(4)]
        GROUP_S = len(S_UNITS)
        PIECES = (((0, 0),), ((0, 1), (384, 3)), ((0, 2),))
        PIECE_AT, PIECE_N = (0, 512, 1024), (512, 512, 256)
        KEY_AT = (0, 512, 1024, 512 + 384)
        GROUP_ST = PER_KV * len(PIECES)
        ROPE_TILES = [K0, K0 + 1] + [query_tile(n) for n in range(KV_HEADS)]

        block = ctx.enter_context(nc.Block())

        @block.sync
        def _(sp):
            sp.dma_start(c16[:, :], const16).then_inc(const_in, 16)
            sp.dma_start(c32[:, :], const32).then_inc(const_in, 16)
            sp.dma_start(rot[:, :, :], rotary).then_inc(const_in, 16)
            for kv in range(KV_HEADS):
                sp.dma_start(k_stack[96:128, kv, :], const16[96:128, 4 * P:]).then_inc(indicator_in, 16)
            def load_x(b):
                for kt in range(KT):
                    sp.wait_ge(x_lo, b * KT + kt + 1)
                    hold(sp, passed)
                    sp.dma_start(xin[:, kt % 4, :], xT[b, kt * P:(kt + 1) * P, :]).then_inc(x_loaded[kt % 4], 16)

            load_x(0)
            for u in range(2 * KT):
                if u >= W_SLOTS:
                    sp.wait_ge(w_lo, u - W_SLOTS + 1)
                kt, s = u % KT, u % W_SLOTS
                src = wqkvT[kt * P:(kt + 1) * P, :] if u < KT else woT[kt * P:(kt + 1) * P, :]
                sp.dma_start(w_in[:, s * QKV:s * QKV + src.shape[1]], src).then_inc(w_loaded[s], 16)

            def batch(b, more):
                for n in range(2 + KV_HEADS):
                    s = n % 2
                    sp.wait_ge(stage_full, b * 10 + n + 1)
                    hold(sp, passed)
                    if n == 0:
                        sp.wait_ge(st_done, b * (KV_HEADS * GROUP_ST) + ST_CREDIT)
                    if n >= 2:
                        sp.wait_ge(st_done, b * (KV_HEADS * GROUP_ST) + (n - 2 - 3) * GROUP_ST + ST_CREDIT)
                    for j in range(PER_KV):
                        for row, part in enumerate((0, 0, 1) if n < 2 else (0, 1, 0)):
                            to = (k_stack[32 * row:32 * row + 32, PER_KV * n + j, :] if n < 2 else
                                  q_stack[32 * row:32 * row + 32, (n - 2) % 4, j, :])
                            sp.dma_start(to, stage[32 * j:32 * j + 32, s, part, :]).then_inc(stage_sent[s], 16)
                if more:
                    load_x(b + 1)
                for t in range(SEQ_TILES):
                    s = t % 2
                    if t < 2:
                        sp.wait_ge(y_stored[s], b * 32 + 16)
                        hold(sp, passed)
                        sp.dma_start(y[:, s, :], x[b, t * P:(t + 1) * P, :]).then_inc(y_loaded[s], 16)
                for t in range(SEQ_TILES):
                    s = t % 2
                    sp.wait_ge(y_done, b * SEQ_TILES + t + 1)
                    hold(sp, passed)
                    sp.dma_start(x1[b, t * P:(t + 1) * P, :], y[:, s, :]).then_inc(y_stored[s], 16)
                    if t + 2 < SEQ_TILES:
                        sp.wait_ge(y_stored[s], b * 32 + 32)
                        hold(sp, passed)
                        sp.dma_start(y[:, s, :], x[b, (t + 2) * P:(t + 3) * P, :]).then_inc(y_loaded[s], 16)

            batches(sp, batch)
            for s in range(2):
                sp.wait_ge(y_stored[s], 16 + BATCH * 32)

        @block.gpsimd
        def _(pool):
            pool.sem_inc(st_done, ST_CREDIT)
            pool.sem_inc(proj_done, PROJ_CREDIT)
            pool.sem_inc(bias_turned, ONE)
            pool.sem_inc(pv_done, ONE)
            pool.sem_inc(ot_done, ONE)
            pool.sem_inc(edge_done, EDGE_CREDIT)
            for s in range(2):
                pool.sem_inc(stage_sent[s], STAGE_COUNT)
                pool.sem_inc(y_stored[s], 16)
            nc.gpsimd.memset(power[:, :], -0.5).then_inc(pool_set, 1)
            nc.gpsimd.memset(ones[:, :], 1.0).then_inc(pool_set, 1)
            nc.gpsimd.memset(zero[:, :], 0.0).then_inc(pool_set, 1)
            nc.gpsimd.memset(bias[:, :, :, :], 0.0).then_inc(pool_set, 1)
            pool.wait_ge(pool_set, 4)

            def batch(b, more):
                def rotate(n):
                    pool.wait_ge(proj_read, b * PROJ + ROPE_TILES[n] + 1 + PROJ_READ_CREDIT)
                    nc.gpsimd.tensor_tensor(r_sin[:, :], r_sin[:, :], rot[:, 1, :], ALU.mult).then_inc(sin_done, 1)
                    pool.wait_ge(sin_done, b * 10 + n + 1)
                    nc.gpsimd.tensor_tensor(r_out[:, :], r_cos[:, :], r_sin[:, :], ALU.add).then_inc(rotated, 1)
                    pool.wait_ge(rot_hi, b * 10 + n + 1)
                    nc.gpsimd.tensor_tensor(stage[:, n % 2, 1, :], r_out[:, :], stage[:, n % 2, 0, :], ALU.subtract).then_inc(stage_full, 1)

                def edges(g):
                    for i in (2, 3):
                        pool.wait_ge(edge_ready, b * (2 * KV_HEADS) + 2 * g + i - 1)
                        pool.wait_ge(st_done, b * (KV_HEADS * GROUP_ST) + (g - 1) * GROUP_ST + ST_CREDIT)
                        nc.gpsimd.tensor_tensor(edge_diag[:, g % 2, i - 2, :, :], ident.unsqueeze(1).broadcast_to([P, PER_KV, P]),
                                                edge[:, i % 2, :].unsqueeze(2).broadcast_to([P, PER_KV, P]), ALU.mult).then_inc(edge_done, 1)

                def low(g):
                    pool.wait_ge(o_done, b * KV_HEADS + g + 1)
                    nc.gpsimd.tensor_tensor(ot[1][:, g, :], o_norm[:, :], ot[0][:, g, :], ALU.subtract).then_inc(ot_done, 1)

                for n in range(3):
                    rotate(n)
                edges(0)
                for n in range(3, 5):
                    rotate(n)
                for g in range(KV_HEADS):
                    if g:
                        low(g - 1)
                    if g + 1 < KV_HEADS:
                        edges(g + 1)
                    if g + 3 < KV_HEADS:
                        rotate(g + 5)
                low(KV_HEADS - 1)
                for t in range(SEQ_TILES):
                    s = t % 2
                    pool.wait_ge(var_done, b * SEQ_TILES + t + 1)
                    nc.gpsimd.tensor_tensor(rstd[:, s:s + 1], var_eps[:, s:s + 1], power[:, :], ALU.pow).then_inc(rstd_done, 1)

            batches(pool, batch)

        @block.scalar
        def _(act):
            def split_x(b):
                act.wait_ge(proj_done, b * PROJ + 1)
                for kt in range(KT):
                    act.wait_ge(x_loaded[kt % 4], b * 32 + 16 * (kt // 4 + 1))
                    nc.scalar.activation(xs[0][:, kt, :], xin[:, kt % 4, :], ACT.Copy).then_inc(x_hi, 1)

            act.sem_inc(exp_done, EXP_CREDIT)
            split_x(0)
            for u in range(2 * KT):
                kt, s = u % KT, u % W_SLOTS
                w16 = wqkv[0] if u < KT else wo[0]
                act.wait_ge(w_loaded[s], 16 * (u // W_SLOTS + 1))
                nc.scalar.activation(w16[:, kt, :], w_in[:, s * QKV:s * QKV + w16.shape[2]], ACT.Copy, scale=W_SCALE).then_inc(w_hi, 1)

            def batch(b, more):
                def rotated_hi(n):
                    act.wait_ge(rotated, b * 10 + n + 1)
                    act.wait_ge(stage_sent[n % 2], b * (5 * STAGE_COUNT) + (n // 2 + 1) * STAGE_COUNT)
                    nc.scalar.activation(stage[:, n % 2, 0, :], r_out[:, :], ACT.Copy).then_inc(rot_hi, 1)

                for n in range(5):
                    rotated_hi(n)
                for g in range(KV_HEADS):
                    slot = g % 4
                    act.wait_ge(bias_turned, b * (2 * KV_HEADS) + 2 * g + 1 + ONE)
                    nc.scalar.activation(q_stack[96:128, slot, 0:2, :], bias_t[0][96:128, :].rearrange("p (j n) -> p j n", j=2),
                                         ACT.Copy).then_inc(bias_in_a, 1)
                    act.wait_ge(pv_done, b * KV_HEADS + g + ONE)
                    for j in range(PER_KV):
                        for k in range(len(PIECES)):
                            u = j * len(PIECES) + k
                            act.wait_ge(st_done, b * (KV_HEADS * GROUP_ST) + g * GROUP_ST + u + 1 + ST_CREDIT)
                            nc.scalar.activation(probs[:, j, PIECE_AT[k]:PIECE_AT[k] + PIECE_N[k]], st_bank[u % 2][:, 0:PIECE_N[k]],
                                                 ACT.Exp, scale=float(HD) ** -0.5).then_inc(exp_done, 1)
                    if g + 3 < KV_HEADS:
                        rotated_hi(g + 5)
                if more:
                    split_x(b + 1)

            batches(act, batch)

        @block.tensor
        def _(pe):
            def product(out, lhs, rhs, n):
                def one(i):
                    kt, (a, c) = i // 3, PARTS[i % 3]
                    return nc.tensor.matmul(out, lhs(a, kt), rhs(c, kt), start=(i == 0), stop=(i == 3 * KT - 1))
                return [lambda i=i: one(i) for i in range(n)]

            pe.wait_ge(const_in, 48)
            pe.wait_ge(indicator_in, 16 * KV_HEADS)
            pe.wait_ge(pool_set, 4)
            pe.wait_ge(w_lo, KT)

            def batch(b, more):
                def proj_room(p):
                    back = 1 if Q1 < p <= Y0 else 2
                    pe.wait_ge(proj_read, b * PROJ + p - back + 1 + PROJ_READ_CREDIT)

                def proj(p, passes):
                    proj_room(p)
                    for f in passes[:-1]:
                        f()
                    passes[-1]().then_inc(proj_done, 1)

                def head_tile(p, c):
                    return product(proj_bank(p)[:, :], lambda a, kt: wqkv[a][:, kt, c * P:(c + 1) * P],
                                   lambda a, kt: xs[a][:, kt, :], 3 * KT)

                def scores(g, u):
                    i, heads = S_UNITS[u]
                    pe.wait_ge(s_read, b * (KV_HEADS * GROUP_S) + g * GROUP_S + u + 1)
                    n, out = P * (i + 1), s_bank[(g * GROUP_S + u) % 3]
                    for k, j in enumerate(heads):
                        nc.tensor.matmul(out[:, k * n:(k + 1) * n], q_stack[0:96, g % 4, j, P * i:n], k_stack[0:96, g, 0:n],
                                         start=(k == 0), stop=True, skip_group_check=True)
                        last = nc.tensor.matmul(out[:, (k + 1) * n - P:(k + 1) * n], ident, causal_qk, start=False, stop=True,
                                                skip_group_check=True)
                    last.then_inc(s_done, 1)

                def values(g):
                    calls = []
                    for kb in range(SEQ_TILES):
                        for bank_, lhs in ((o_bank, v[:, kb, HD * g:HD * (g + 1)]), (sum_bank, ones[:, :])):
                            def one(kb=kb, bank_=bank_, lhs=lhs):
                                for j in range(PER_KV):
                                    last = nc.tensor.matmul(bank_[32 * j:32 * j + 32, P * kb:SEQ], lhs,
                                                            probs[:, j, KEY_AT[kb]:KEY_AT[kb] + SEQ - P * kb],
                                                            start=(kb == 0), stop=True, skip_group_check=True)
                                return last
                            calls.append(one)
                    return calls

                def begin_scores(g):
                    pe.wait_ge(stage_sent[g % 2], b * (5 * STAGE_COUNT) + ((2 + g) // 2 + 2) * STAGE_COUNT)

                def scores_by_key(g, j, k):
                    u = j * len(PIECES) + k
                    pe.wait_ge(exp_done, b * (KV_HEADS * GROUP_ST) + g * GROUP_ST + u - 1 + EXP_CREDIT)
                    out = st_bank[u % 2]
                    for at, kb in PIECES[k]:
                        nc.tensor.matmul(out[:, at:at + SEQ - P * kb], k_stack[:, g, P * kb:P * (kb + 1)],
                                         q_stack[:, g % 4, j, P * kb:SEQ], start=(at == 0), stop=True, skip_group_check=True)
                        last = nc.tensor.matmul(out[:, at:at + P], ident, causal_kq, start=False, stop=True, skip_group_check=True)
                        if kb in (1, 2):
                            last = nc.tensor.matmul(out[:, at + P:at + 2 * P], same_chunk, edge_diag[:, g % 2, kb - 1, j, :],
                                                    start=False, stop=True, skip_group_check=True)
                    last.then_inc(st_done, 1)

                def begin_values(g):
                    pe.wait_ge(exp_done, b * (KV_HEADS * GROUP_ST) + (g + 1) * GROUP_ST + EXP_CREDIT)
                    pe.wait_ge(o_read, b * KV_HEADS + g + ONE)

                pe.wait_ge(x_lo, b * KT + KT + X_CREDIT)
                for n in range(2):
                    proj(K0 + n, head_tile(K0 + n, KT + n))
                proj(Q0, head_tile(Q0, 0))
                for t in range(SEQ_TILES):
                    p = V0 + t
                    proj(p, product(proj_bank(p)[:, 0:KV], lambda a, kt, t=t: xs[a][:, kt, t * P:(t + 1) * P],
                                    lambda a, kt: wqkv[a][:, kt, HID + KV:QKV], 3 * KT))
                begin_scores(0)
                pe.wait_ge(proj_read, b * PROJ + V0 + SEQ_TILES + PROJ_READ_CREDIT)
                first = list(range(GROUP_S))
                for n in range(1, 3):
                    p = query_tile(n)
                    proj_room(p)
                    passes = head_tile(p, n)
                    for k, f in enumerate(passes):
                        last = f()
                        if k == len(passes) - 1:
                            last.then_inc(proj_done, 1)
                        if k % 4 == 3 and first:
                            scores(0, first.pop(0))
                for g in range(KV_HEADS):
                    query = head_tile(query_tile(g + 3), g + 3) if g + 3 < KV_HEADS else []
                    value = values(g - 1) if g else []
                    ahead = list(range(GROUP_S)) if g + 1 < KV_HEADS else []

                    def scores_ahead(n):
                        for _ in range(n):
                            if ahead:
                                u = ahead.pop(0)
                                if u == 0:
                                    begin_scores(g + 1)
                                scores(g + 1, u)

                    scores_ahead(2)
                    pe.wait_ge(bias_done, b * (KV_HEADS * SEQ_TILES) + SEQ_TILES * (g + 1))
                    pe.wait_ge(exp_done, b * (KV_HEADS * GROUP_ST) + g * GROUP_ST + EXP_CREDIT)
                    for k in range(2):
                        for jj in range(2):
                            for i in range(SEQ_TILES):
                                at = jj * SEQ + i * P
                                last = nc.tensor.transpose(bias_t[k][96:128, at:at + P], bias[:, i, 2 * k + jj, :], ident)
                        last.then_inc(bias_turned, 1)
                    if value:
                        begin_values(g - 1)
                        for n, f in enumerate(value):
                            last = f()
                            if n == len(value) - 1:
                                last.then_inc(pv_done, 1)
                            if n in (3, 7):
                                scores_ahead(1)
                    pe.wait_ge(bias_in_a, b * KV_HEADS + g + 1)
                    pe.wait_ge(bias_in_d, b * KV_HEADS + g + 1)
                    pe.wait_ge(edge_done, b * (2 * KV_HEADS) + 2 * g + 2 + EDGE_CREDIT)
                    if query:
                        proj_room(query_tile(g + 3))
                    for u in range(GROUP_ST):
                        scores_by_key(g, *divmod(u, len(PIECES)))
                        for f in query[2 * u:2 * u + 2]:
                            last = f()
                        if query and u == GROUP_ST - 1:
                            last.then_inc(proj_done, 1)
                        if u % 3 != 2:
                            scores_ahead(1)
                    scores_ahead(GROUP_S)
                begin_values(KV_HEADS - 1)
                for f in values(KV_HEADS - 1):
                    last = f()
                last.then_inc(pv_done, 1)
                pe.wait_ge(w_lo, 2 * KT)
                pe.wait_ge(ot_done, b * KV_HEADS + KV_HEADS + ONE)
                for t in range(SEQ_TILES):
                    for h in range(2):
                        p = Y0 + 2 * t + h
                        proj(p, product(proj_bank(p)[:, :], lambda a, kt, t=t: ot[a][:, kt, t * P:(t + 1) * P],
                                        lambda a, kt, h=h: wo[a][:, kt, h * 512:(h + 1) * 512], 3 * KT))

            batches(pe, batch)

        @block.vector
        def _(dve):
            def split_x(b):
                for kt in range(KT):
                    dve.wait_ge(x_hi, b * KT + kt + 1)
                    nc.vector.tensor_tensor(xs[1][:, kt, :], xin[:, kt % 4, :], xs[0][:, kt, :], ALU.subtract).then_inc(x_lo, 1)

            dve.sem_inc(x_lo, X_CREDIT)
            split_x(0)
            for u in range(2 * KT):
                kt, s = u % KT, u % W_SLOTS
                w16 = wqkv if u < KT else wo
                w32 = w_in[:, s * QKV:s * QKV + w16[0].shape[2]]
                dve.wait_ge(w_hi, u + 1)
                nc.vector.scalar_tensor_tensor(out=w16[1][:, kt, :], in0=w32, scalar=W_SCALE, in1=w16[0][:, kt, :],
                                               op0=ALU.mult, op1=ALU.subtract).then_inc(w_lo, 1)
            dve.sem_inc(proj_read, PROJ_READ_CREDIT)
            dve.sem_inc(s_read, S_CREDIT)
            dve.sem_inc(o_read, ONE)
            dve.wait_ge(const_in, 48)
            dve.wait_ge(pool_set, 4)

            def batch(b, more):
                steps = [0]

                def step(ins):
                    steps[0] += 1
                    ins.then_inc(dve_step, 1)

                def stepped():
                    dve.wait_ge(dve_step, b * DVE_STEPS + steps[0])

                def rotate(p):
                    tile = proj_bank(p)[:, :]
                    dve.wait_ge(proj_done, b * PROJ + p + 1 + PROJ_CREDIT)
                    if p != K0:
                        dve.wait_ge(rotated, b * 10 + ROPE_TILES.index(p))
                    nc.vector.tensor_tensor(r_cos[:, :], tile, rot[:, 0, :], ALU.mult)
                    nc.vector.stream_shuffle(out=r_sin[:, :], in_=tile, mask=[(i + HD // 2) % HD for i in range(HD)]).then_inc(proj_read, 1)

                def row_tile(g, i):
                    n = BLOCK_CHUNKS * (i + 1)
                    s = i % 2
                    cm = chunk_max[:, s, :, 0:n]
                    units = [u for u in range(GROUP_S) if S_UNITS[u][0] == i]
                    for u in units:
                        heads = S_UNITS[u][1]
                        width = len(heads) * n * CHUNK
                        dve.wait_ge(s_done, b * (KV_HEADS * GROUP_S) + g * GROUP_S + u + 1)
                        nc.vector.tensor_reduce(chunk_max[:, s, heads[0]:heads[-1] + 1, 0:n],
                                                s_bank[(g * GROUP_S + u) % 3][:, 0:width].rearrange("p (h c k) -> p h c k", h=len(heads), k=CHUNK),
                                                AX.X, ALU.max).then_inc(s_read, 1)
                    dve.wait_ge(s_read, b * (KV_HEADS * GROUP_S) + g * GROUP_S + units[-1] + 1 + S_CREDIT)
                    hold(dve, passed)
                    for j in range(PER_KV):
                        last = nc.vector.max(top8[:, s, j, :], chunk_max[:, s, j, 0:n])
                    step(last)
                    stepped()
                    row_max = top8[:, s, :, 0:1].broadcast_to([P, PER_KV, n])
                    source = zero[:, 0:n].unsqueeze(1).broadcast_to([P, PER_KV, n])
                    if i >= 2:
                        hold(dve, passed)
                        for j in range(PER_KV):
                            last = nc.vector.match_replace(left[:, s, j, 0:n], top8[:, s, j, :], chunk_max[:, s, j, 0:n], TAKEN)
                        step(last)
                        stepped()
                        far = c32[:, (i - 2) * N_CHUNKS:(i - 2) * N_CHUNKS + n].unsqueeze(1).broadcast_to([P, PER_KV, n])
                        own = c32[:, 2 * N_CHUNKS:2 * N_CHUNKS + BLOCK_CHUNKS].unsqueeze(1).broadcast_to([P, PER_KV, BLOCK_CHUNKS])
                        nc.vector.scalar_tensor_tensor(out=pen[:, s, :, 0:n], in0=left[:, s, :, 0:n], scalar=TAKEN_OVER, in1=far,
                                                       op0=ALU.is_lt, op1=ALU.mult)
                        step(nc.vector.scalar_tensor_tensor(out=pen_edge[:, s, :, :], in0=left[:, s, :, BLOCK_CHUNKS * (i - 1):BLOCK_CHUNKS * i],
                                                            scalar=TAKEN_OVER, in1=own, op0=ALU.is_lt, op1=ALU.mult))
                        stepped()
                        dve.wait_ge(edge_done, b * (2 * KV_HEADS) + 2 * g + i - 1 - 2 + EDGE_CREDIT)
                        nc.vector.tensor_reduce(edge[:, s, :], pen_edge[:, s, :, :], AX.X, ALU.add).then_inc(edge_ready, 1)
                        source = pen[:, s, :, 0:n]
                    if i == 0:
                        dve.wait_ge(bias_turned, b * (2 * KV_HEADS) + 2 * g + ONE)
                    nc.vector.tensor_tensor(bias[:, i, :, 0:n], source, row_max, ALU.subtract).then_inc(bias_done, 1)
                def normalise(g):
                    dve.wait_ge(pv_done, b * KV_HEADS + g + 1 + ONE)
                    step(nc.vector.transpose(sum_turned[:, :], sum_bank[:, :]))
                    stepped()
                    step(nc.vector.reciprocal(inv_turned[:, :], sum_turned[:, ::32]))
                    stepped()
                    step(nc.vector.transpose(row_inv[:, :], inv_turned[:, :].unsqueeze(2).broadcast_to([P, SEQ // 32, 32])))
                    stepped()
                    dve.wait_ge(ot_done, b * KV_HEADS + g + ONE)
                    nc.vector.tensor_tensor(o_norm[:, :], o_bank[:, :], row_inv[:, :], ALU.mult).then_inc(o_read, 1)
                    dve.wait_ge(o_read, b * KV_HEADS + g + 1 + ONE)
                    if g == 0:
                        dve.wait_ge(proj_done, b * PROJ + PROJ_CREDIT)
                    nc.vector.tensor_copy(ot[0][:, g, :], o_norm[:, :]).then_inc(o_done, 1)

                for p in ROPE_TILES[0:3]:
                    rotate(p)
                for t in range(SEQ_TILES):
                    p = V0 + t
                    dve.wait_ge(proj_done, b * PROJ + p + 1 + PROJ_CREDIT)
                    if t == 0:
                        dve.wait_ge(pv_done, b * KV_HEADS + ONE)
                    nc.vector.tensor_copy(v[:, t, :], proj_bank(p)[:, 0:KV]).then_inc(proj_read, 1)
                row_tile(0, 0)
                row_tile(0, 1)
                rotate(query_tile(1))
                row_tile(0, 2)
                row_tile(0, 3)
                rotate(query_tile(2))
                for g in range(KV_HEADS):
                    ahead = g + 1 < KV_HEADS
                    if ahead:
                        row_tile(g + 1, 0)
                    dve.wait_ge(bias_turned, b * (2 * KV_HEADS) + 2 * g + 2 + ONE)
                    nc.vector.tensor_copy(q_stack[96:128, g % 4, 2:4, :], bias_t[1][96:128, :].rearrange("p (j n) -> p j n", j=2)).then_inc(bias_in_d, 1)
                    if ahead:
                        row_tile(g + 1, 1)
                    if g:
                        normalise(g - 1)
                    if ahead:
                        row_tile(g + 1, 2)
                        row_tile(g + 1, 3)
                    if g + 3 < KV_HEADS:
                        rotate(query_tile(g + 3))
                normalise(KV_HEADS - 1)
                if more:
                    split_x(b + 1)
                for t in range(SEQ_TILES):
                    s = t % 2
                    dve.wait_ge(y_loaded[s], b * 32 + 16 * (t // 2 + 1))
                    for h in range(2):
                        p = Y0 + 2 * t + h
                        half = y[:, s, h * 512:(h + 1) * 512]
                        dve.wait_ge(proj_done, b * PROJ + p + 1 + PROJ_CREDIT)
                        nc.vector.scalar_tensor_tensor(out=half, in0=proj_bank(p)[:, :], scalar=1.0 / (W_SCALE * W_SCALE), in1=half,
                                                       op0=ALU.mult, op1=ALU.add).then_inc(proj_read, 1)
                        dve.wait_ge(proj_read, b * PROJ + p + 1 + PROJ_READ_CREDIT)
                        step(nc.vector.bn_stats(stats[:, s, h, :], half))
                    stepped()
                    hold(dve, passed)
                    step(nc.vector.bn_aggr(mean_var[:, s, :], stats[:, s, :, :].rearrange("p a b -> p (a b)")))
                    stepped()
                    nc.vector.tensor_scalar(var_eps[:, s:s + 1], mean_var[:, s, 1:2], EPS, None, ALU.add).then_inc(var_done, 1)
                    dve.wait_ge(rstd_done, b * SEQ_TILES + t + 1)
                    nc.vector.tensor_scalar(y[:, s, :], y[:, s, :], mean_var[:, s, 0:1], rstd[:, s:s + 1], ALU.subtract,
                                            ALU.mult).then_inc(y_done, 1)
                assert steps[0] == DVE_STEPS, steps

            batches(dve, batch)


DVE_STEPS = KV_HEADS * (4 * 1 + 2 * 2) + KV_HEADS * 3 + SEQ_TILES * 3


def mlp(nc, x1, w_units, z_units, s_units, ident32, out):
    with ExitStack() as ctx:
        sb = lambda name, shape, dt: ctx.enter_context(nc.sbuf_tensor(name, shape, dt))
        sem = lambda name: ctx.enter_context(nc.semaphore(name))

        TILES = TOK // P
        TT = TOK // 512
        x1s = [sb(f"x1s{p}", [P, KT, TOK], F16) for p in range(2)]
        acc = sb("acc", [P, TILES, HID], F32)
        wset = [[sb(f"wset{s}{p}", [P, UNITS, UW], F16) for p in range(2)] for s in range(2)]
        w_raw = sb("w_raw", [P, 2, UW], I32)
        rows = sb("rows", [P, UW], F32)
        z_all = sb("z_all", [P, 2, UW], I32)
        s_all = sb("s_all", [P, 2, UW], F32)
        silu = sb("silu", [P, 2, 512], F32)
        hidden = sb("hidden", [P, 2, 512], F32)
        hs = [sb(f"hs{p}", [P, 2, 2, 512], F16) for p in range(2)]
        ident = hidden[:, 0, 0:P]
        stats = sb("stats2", [P, 4, 2, 6], F32)
        mean_var = sb("mean_var2", [P, 4, 2], F32)
        var_eps = sb("var_eps2", [P, 4], F32)
        rstd = sb("rstd2", [P, 4], F32)
        power = sb("power2", [P, 4], F32)
        bank = [ctx.enter_context(nc.psum_tensor(f"mbank{i}", [P, 512], F32)) for i in range(8)]
        gate_bank, up_bank, down_bank = bank[0:4:2], bank[1:4:2], bank[4:8]

        ident_in = sem("ident_in")
        acc_in = [sem(f"acc_in{k}") for k in range(TT)]
        turned = sem("turned")
        turned_hi = sem("turned_hi")
        turned_read = sem("turned_read")
        unit_in = [sem(f"unit_in{s}") for s in range(2)]
        spread = sem("spread")
        centred = sem("centred")
        scaled = sem("scaled")
        unit_hi = sem("unit_hi")
        unit_lo = sem("unit_lo")
        gu_done = sem("gu_done")
        silu_done = sem("silu_done")
        glu_done = sem("glu_done")
        h_hi = sem("h_hi")
        h_lo = sem("h_lo")
        down_done = sem("down_done")
        acc_done = sem("acc_done")
        stats_done = sem("stats_done")
        var_done = sem("var_done2")
        rstd_done = sem("rstd_done2")
        out_done = sem("out_done")
        stored = sem("stored")
        power_set = sem("power_set")
        passed = sem("passed2")

        DOWN_CREDIT = 33
        TILE_DOWNS = 8
        CHUNK_DOWNS = TT * TILE_DOWNS
        GLUS = 2 * TT
        PAIRS = MLP_CHUNKS // 2
        x1_rows = x1.rearrange("b (t p) h -> p (b t) h", p=P)
        out_rows = out.rearrange("b (t p) h -> p (b t) h", p=P)

        def pairs(eng, body):
            with eng.Fori(0, PAIRS - 1) as i:
                body(i * 2, 0, True)
                body(i * 2 + 1, 1, True)
            body(MLP_CHUNKS - 2, 0, True)
            body(MLP_CHUNKS - 1, 1, False)

        ORDER = (("glu", 0), ("glu", 1), ("down", 0), ("glu", 2), ("down", 1), ("glu", 3), ("down", 2), ("down", 3))
        BEHIND = {("glu", 0): (0, 1), ("glu", 1): (2, 3), ("down", 0): (4,), ("glu", 2): (5, 6), ("down", 1): (7,),
                  ("glu", 3): (8, 9), ("down", 2): (10,), ("down", 3): (11,)}

        block = ctx.enter_context(nc.Block())

        @block.sync
        def _(sp):
            def load_unit(c, k):
                s = k % 2
                sp.wait_ge(unit_lo, c * UNITS + k + 1)
                hold(sp, passed)
                sp.dma_start(w_raw[:, s, :], w_units[c, k]).then_inc(unit_in[s], 16)
                sp.dma_start(rows[64 * s:64 * s + 1, :], z_units[c, k:k + 1, :].bitcast(F32)).then_inc(unit_in[s], 16)
                sp.dma_start(rows[64 * s + 32:64 * s + 33, :], s_units[c, k:k + 1, :]).then_inc(unit_in[s], 16)

            sp.dma_start(ident, ident32).then_inc(ident_in, 16)
            for k in range(TT):
                sp.dma_start(acc[:, 4 * k:4 * k + 4, :], x1_rows[:, 4 * k:4 * k + 4, :]).then_inc(acc_in[k], 16)
            with sp.Fori(0, MLP_CHUNKS) as c:
                for k in range(UNITS):
                    load_unit(c, k)
            for t in range(TILES):
                sp.wait_ge(out_done, t + 1)
                sp.dma_start(out_rows[:, t, :], acc[:, t, :]).then_inc(stored, 16)
            sp.wait_ge(stored, 16 * TILES)

        @block.gpsimd
        def _(pool):
            pool.sem_inc(down_done, DOWN_CREDIT)
            nc.gpsimd.memset(power[:, :], -0.5).then_inc(power_set, 1)
            with pool.Fori(0, MLP_CHUNKS) as c:
                for k in range(UNITS):
                    s = k % 2
                    pool.wait_ge(unit_in[s], c * (48 * UNITS // 2) + 48 * (k // 2 + 1))
                    pool.wait_ge(scaled, c * UNITS + k + 1)
                    hold(pool, passed)
                    nc.gpsimd.partition_broadcast(z_all[:, s, :], rows[64 * s:64 * s + 1, :].bitcast(I32), channels=P).then_inc(spread, 1)
                    nc.gpsimd.partition_broadcast(s_all[:, s, :], rows[64 * s + 32:64 * s + 33, :], channels=P).then_inc(spread, 1)
            pool.wait_ge(power_set, 1)
            for k in range(TT):
                pool.wait_ge(var_done, k + 1)
                nc.gpsimd.tensor_tensor(rstd[:, :], var_eps[:, :], power[:, :], ALU.pow).then_inc(rstd_done, 1)

        @block.scalar
        def _(act):
            act.sem_inc(glu_done, 2)

            def unit_high(c, s, k):
                if k == 0:
                    act.wait_ge(down_done, c * CHUNK_DOWNS + 1)
                act.wait_ge(scaled, c * UNITS + k + 1 + 2)
                nc.scalar.activation(wset[s][0][:, k, :], w_raw[:, k % 2, :].bitcast(F32), ACT.Copy).then_inc(unit_hi, 1)

            for k in range(UNITS):
                unit_high(0, 0, k)
            for r in range(2 * TILES):
                t, h = divmod(r, 2)
                act.wait_ge(turned, r + 1)
                nc.scalar.activation(x1s[0][:, 4 * h:4 * h + 4, t * P:(t + 1) * P], down_bank[r % 4][:, :].rearrange("p (k t) -> p k t", k=4),
                                     ACT.Copy, scale=X1_SCALE).then_inc(turned_hi, 1)

            def chunk(c, s, more):
                for kind, tt in ORDER:
                    behind = BEHIND[kind, tt] if more else ()
                    if kind == "glu":
                        for j in range(2):
                            n = 2 * tt + j
                            act.wait_ge(gu_done, c * GLUS + n + 1)
                            act.wait_ge(glu_done, c * GLUS + n + 1)
                            nc.scalar.activation(silu[:, j, :], gate_bank[j][:, :], ACT.Silu, scale=1.0 / (W_SCALE * X1_SCALE)).then_inc(silu_done, 1)
                            act.wait_ge(glu_done, c * GLUS + n + 1 + 2)
                            act.wait_ge(down_done, c * CHUNK_DOWNS + TILE_DOWNS * (tt - 1) + DOWN_CREDIT)
                            nc.scalar.activation(hs[0][:, tt % 2, j, :], hidden[:, j, :], ACT.Copy).then_inc(h_hi, 1)
                            if behind:
                                unit_high(c + 1, 1 - s, behind[j])
                    elif behind:
                        unit_high(c + 1, 1 - s, behind[0])

            pairs(act, chunk)

        @block.tensor
        def _(pe):
            pe.wait_ge(ident_in, 16)
            for r in range(2 * TILES):
                t, h = divmod(r, 2)
                if r % 8 == 0:
                    pe.wait_ge(acc_in[r // 8], 16)
                if r >= 4:
                    pe.wait_ge(turned_read, r - 3)
                for k in range(4):
                    last = nc.tensor.transpose(down_bank[r % 4][:, k * P:(k + 1) * P], acc[:, t, (4 * h + k) * P:(4 * h + k + 1) * P], ident)
                last.then_inc(turned, 1)
            pe.wait_ge(turned_read, 2 * TILES)

            def chunk(c, s, more):
                for kind, tt in ORDER:
                    if kind == "glu":
                        for j in range(2):
                            n = 2 * tt + j
                            if n == 0:
                                pe.wait_ge(unit_lo, c * UNITS + 8 + 2)
                            pe.wait_ge(glu_done, c * GLUS + n + 1)
                            for first, to in ((0, gate_bank), (4, up_bank)):
                                for i in range(3 * KT):
                                    kt, (a, x) = i // 3, PARTS[i % 3]
                                    last = nc.tensor.matmul(to[j][:, :], wset[s][a][:, first + kt // 2, (kt % 2) * IC + j * P:(kt % 2) * IC + (j + 1) * P],
                                                            x1s[x][:, kt, 512 * tt:512 * (tt + 1)], start=(i == 0), stop=(i == 3 * KT - 1))
                            last.then_inc(gu_done, 1)
                    else:
                        if tt == 0:
                            pe.wait_ge(unit_lo, c * UNITS + UNITS + 2)
                        pe.wait_ge(h_lo, c * GLUS + 2 * tt + 2)
                        for m in range(TILE_DOWNS):
                            tl, h = divmod(m, 2)
                            pe.wait_ge(acc_done, c * CHUNK_DOWNS + TILE_DOWNS * tt + m + 1)
                            for i in range(6):
                                j, (a, w) = i // 3, PARTS[i % 3]
                                last = nc.tensor.matmul(down_bank[m % 4][:, :], hs[a][:, tt % 2, j, tl * P:(tl + 1) * P],
                                                        wset[s][w][:, 8 + 2 * j + h, :], start=(i == 0), stop=(i == 5))
                            last.then_inc(down_done, 1)

            pairs(pe, chunk)

        @block.vector
        def _(dve):
            dve.sem_inc(unit_lo, 2)
            dve.sem_inc(scaled, 2)
            dve.sem_inc(acc_done, 4)

            def unit_scale(c, k):
                s = k % 2
                raw, w = w_raw[:, s, :], w_raw[:, s, :].bitcast(F32)
                dve.wait_ge(spread, c * (2 * UNITS) + 2 * k + 2)
                dve.wait_ge(unit_in[s], c * (48 * UNITS // 2) + 48 * (k // 2 + 1))
                nc.vector.tensor_tensor(w, raw, z_all[:, s, :], ALU.subtract).then_inc(centred, 1)
                dve.wait_ge(centred, c * UNITS + k + 1)
                nc.vector.scalar_tensor_tensor(out=w, in0=w, scalar=W_SCALE, in1=s_all[:, s, :], op0=ALU.mult, op1=ALU.mult).then_inc(scaled, 1)

            def unit_low(c, s, k):
                dve.wait_ge(unit_hi, c * UNITS + k + 1)
                nc.vector.tensor_tensor(wset[s][1][:, k, :], w_raw[:, k % 2, :].bitcast(F32), wset[s][0][:, k, :], ALU.subtract).then_inc(unit_lo, 1)

            for k in range(UNITS):
                unit_scale(0, k)
                if k:
                    unit_low(0, 0, k - 1)
            unit_low(0, 0, UNITS - 1)
            for r in range(2 * TILES):
                t, h = divmod(r, 2)
                dve.wait_ge(turned_hi, r + 1)
                nc.vector.scalar_tensor_tensor(out=x1s[1][:, 4 * h:4 * h + 4, t * P:(t + 1) * P],
                                               in0=down_bank[r % 4][:, :].rearrange("p (k t) -> p k t", k=4), scalar=X1_SCALE,
                                               in1=x1s[0][:, 4 * h:4 * h + 4, t * P:(t + 1) * P], op0=ALU.mult,
                                               op1=ALU.subtract).then_inc(turned_read, 1)

            def chunk(c, s, more):
                for kind, tt in ORDER:
                    behind = BEHIND[kind, tt] if more else ()
                    if kind == "glu":
                        for j in range(2):
                            n = 2 * tt + j
                            dve.wait_ge(silu_done, c * GLUS + n + 1)
                            nc.vector.scalar_tensor_tensor(out=hidden[:, j, :], in0=up_bank[j][:, :], scalar=1.0 / (W_SCALE * X1_SCALE),
                                                           in1=silu[:, j, :], op0=ALU.mult, op1=ALU.mult).then_inc(glu_done, 1)
                            if behind:
                                unit_scale(c + 1, behind[j])
                            dve.wait_ge(h_hi, c * GLUS + n + 1)
                            nc.vector.tensor_tensor(hs[1][:, tt % 2, j, :], hidden[:, j, :], hs[0][:, tt % 2, j, :],
                                                    ALU.subtract).then_inc(h_lo, 1)
                            if behind:
                                unit_low(c + 1, 1 - s, behind[j])
                    else:
                        for m in range(TILE_DOWNS):
                            tl, h = divmod(m, 2)
                            part = acc[:, 4 * tt + tl, 512 * h:512 * (h + 1)]
                            dve.wait_ge(down_done, c * CHUNK_DOWNS + TILE_DOWNS * tt + m + 1 + DOWN_CREDIT)
                            nc.vector.scalar_tensor_tensor(out=part, in0=down_bank[m % 4][:, :], scalar=1.0 / W_SCALE, in1=part,
                                                           op0=ALU.mult, op1=ALU.add).then_inc(acc_done, 1)
                            if behind and m == 2:
                                unit_scale(c + 1, behind[0])
                            if behind and m == 5:
                                unit_low(c + 1, 1 - s, behind[0])
                        if not more:
                            norm(c, tt)

            def norm(c, tt):
                dve.wait_ge(acc_done, c * CHUNK_DOWNS + TILE_DOWNS * (tt + 1) + 4)
                for t in range(4):
                    for h in range(2):
                        nc.vector.bn_stats(stats[:, t, h, :], acc[:, 4 * tt + t, 512 * h:512 * (h + 1)]).then_inc(stats_done, 1)
                dve.wait_ge(stats_done, 16 * tt + 8)
                for t in range(4):
                    nc.vector.bn_aggr(mean_var[:, t, :], stats[:, t, :, :].rearrange("p a b -> p (a b)")).then_inc(stats_done, 2)
                dve.wait_ge(stats_done, 16 * tt + 16)
                nc.vector.tensor_scalar(var_eps[:, :], mean_var[:, :, 1], EPS, None, ALU.add).then_inc(var_done, 1)
                dve.wait_ge(rstd_done, tt + 1)
                for t in range(4):
                    nc.vector.tensor_scalar(acc[:, 4 * tt + t, :], acc[:, 4 * tt + t, :], mean_var[:, t, 0:1], rstd[:, t:t + 1],
                                            ALU.subtract, ALU.mult).then_inc(out_done, 1)

            pairs(dve, chunk)


_OUT = ((BATCH, SEQ, HID), "float32")


def kernel(**inputs):
    import concourse.bacc as _bacc
    from concourse.bass_utils import run_bass_kernel_spmd as _run

    arr = {k: np.asarray(a) for k, a in inputs.items()}
    x = arr["L0_attn_hidden_states"]
    wqkvT = np.concatenate([arr["L0_attn_wq"], arr["L0_attn_wk"], arr["L0_attn_wv"]], axis=0).T

    def wide(w):
        return w.reshape(4, 2, P, MLP_CHUNKS, IC).transpose(3, 0, 2, 1, 4).reshape(MLP_CHUNKS, 4, P, UW)

    def wide_rows(z):
        return z.reshape(4, 2, MLP_CHUNKS, IC).transpose(2, 0, 1, 3).reshape(MLP_CHUNKS, 4, UW)

    def tall(w):
        return w.reshape(MLP_CHUNKS, 2, P, 2, UW).transpose(0, 1, 3, 2, 4).reshape(MLP_CHUNKS, 4, P, UW)

    def tall_rows(z):
        return z.reshape(MLP_CHUNKS, 4, UW)

    g, u, d = "L0_ffn_gate_", "L0_ffn_up_", "L0_ffn_down_"
    rotary, const16, const32 = host_constants()
    arrays = {
        "x": x,
        "xT": x.transpose(0, 2, 1),
        "wqkvT": wqkvT,
        "woT": arr["L0_attn_wo"].T,
        "w_units": np.concatenate([wide(arr[g + "w"]), wide(arr[u + "w"]), tall(arr[d + "w"])], axis=1),
        "z_units": np.concatenate([wide_rows(arr[g + "z"]), wide_rows(arr[u + "z"]), tall_rows(arr[d + "z"])], axis=1),
        "s_units": np.concatenate([wide_rows(arr[g + "s"]), wide_rows(arr[u + "s"]), tall_rows(arr[d + "s"])], axis=1),
        "rotary": rotary,
        "const16": const16,
        "const32": const32,
        "ident32": np.eye(P, dtype=np.float32),
    }
    arrays = {k: np.ascontiguousarray(a) for k, a in arrays.items()}

    nc = _bacc.Bacc("TRN2", target_bir_lowering=False, num_devices=1)
    d_in = {k: nc.dram_tensor(k, a.shape, mybir.dt.from_np(a.dtype), kind="ExternalInput").ap() for k, a in arrays.items()}
    out = nc.dram_tensor("out", _OUT[0], F32, kind="ExternalOutput").ap()
    x1 = nc.dram_tensor("x1", _OUT[0], F32, kind="Internal").ap()
    attention(nc, d_in["xT"], d_in["x"], d_in["wqkvT"], d_in["woT"], d_in["rotary"], d_in["const16"], d_in["const32"], x1)
    mlp(nc, x1, d_in["w_units"], d_in["z_units"], d_in["s_units"], d_in["ident32"], out)
    r = _run(nc, [arrays], core_ids=[0])
    return r.results[0]["out"]
```

```python
from contextlib import ExitStack

import numpy as np

import concourse.bass as bass
from concourse import mybir

F32 = mybir.dt.float32
F16 = mybir.dt.float16
I32 = mybir.dt.int32
ALU = mybir.AluOpType
ACT = mybir.ActivationFunctionType
AX = mybir.AxisListType

P = 128
BATCH, SEQ, HID = 4, 512, 1024
TOK = BATCH * SEQ
HEADS, KV_HEADS = 32, 8
HD = HID // HEADS
PER_KV = HEADS // KV_HEADS
KV = KV_HEADS * HD
QKV = HID + 2 * KV
KT = HID // P
SEQ_TILES = SEQ // P
CHUNK = 16
BLOCK_CHUNKS = P // CHUNK
N_CHUNKS = SEQ // CHUNK
TOP = 8
INNER = 3584
IC = 256
MLP_CHUNKS = INNER // IC
UNITS = 12
UW = 512
EPS = 1e-5
W_SCALE = 256.0
X1_SCALE = 16.0
MASKED = -30000.0
TAKEN = 3.0e38
TAKEN_OVER = 1.0e38
PARTS = ((0, 0), (0, 1), (1, 0))

X_CREDIT = 8
PROJ_READ_CREDIT = 2
S_CREDIT = 3
ST_CREDIT = 37
EXP_CREDIT = 2
ONE = 1
EDGE_CREDIT = 2
W_SLOTS = 3
STAGE_DMAS = 12
STAGE_COUNT = 16 * STAGE_DMAS
RAW_SLOTS = 2
FIRST_SLOTS = 4
SCALED_CREDIT = 2


def hold(eng, passed):
    eng.sem_inc(passed, 1)


def host_constants():
    inv = (np.float32(1.0) / np.float32(10000.0) ** (np.arange(0, HD, 2, dtype=np.float32) / np.float32(HD))).astype(np.float32)
    freq = np.arange(SEQ, dtype=np.float32)[:, None] * inv[None, :]
    both = np.concatenate([freq, freq], axis=1).T
    sign = np.where(np.arange(HD) < HD // 2, -1.0, 1.0)[:, None].astype(np.float32)
    unscale = np.float32(1.0 / W_SCALE)
    cos = np.tile(np.cos(both) * unscale, (PER_KV, 1))
    sin = np.tile(np.sin(both) * sign * unscale, (PER_KV, 1))
    rotary = np.stack([cos, sin], axis=1).astype(np.float32)

    r = np.arange(P)
    c16 = np.zeros((P, 4 * P + SEQ), np.float16)
    c16[:, 0:P] = np.eye(P)
    c16[:, P:2 * P] = np.where(r[None, :] > r[:, None], MASKED, 0)
    c16[:, 2 * P:3 * P] = np.where(r[:, None] > r[None, :], MASKED, 0)
    c16[:, 3 * P:4 * P] = (r[:, None] // CHUNK == r[None, :] // CHUNK) & (r[None, :] <= r[:, None])
    c16[96:128, 4 * P:] = np.arange(SEQ)[None, :] // CHUNK == np.arange(N_CHUNKS)[:, None]

    c32 = np.zeros((P, 3 * N_CHUNKS), np.float32)
    qc = r // CHUNK
    for i in (2, 3):
        for c in range(BLOCK_CHUNKS, BLOCK_CHUNKS * i):
            block, cl = divmod(c, BLOCK_CHUNKS)
            full = np.ones(P, bool) if block < i - 1 else cl < qc
            c32[:, (i - 2) * N_CHUNKS + c] = np.where(full, MASKED, 0)
    for cl in range(BLOCK_CHUNKS):
        c32[:, 2 * N_CHUNKS + cl] = np.where(cl == qc, MASKED, 0)
    return rotary, c16, c32


class ChunkWeights:

    def __init__(self, nc, space, semaphore, w_units, z_units, s_units):
        self.nc = nc
        self.w_units, self.z_units, self.s_units = w_units, z_units, s_units
        at = [0]

        def cut(kib, dt, pattern=None, **sizes):
            piece = space[:, at[0]:at[0] + kib * 512].bitcast(dt)
            at[0] += kib * 512
            return piece.rearrange(pattern, **sizes) if pattern else piece

        first_set = [cut(UNITS * UW * 2 // 1024, F16, "p (u n) -> p u n", u=UNITS) for _ in range(2)]
        self.sets = [first_set, None]
        self.raw = cut(RAW_SLOTS * 2, I32, "p (s n) -> p s n", s=RAW_SLOTS)
        self.rows = cut(2, F32)
        self.z_all = cut(4, I32, "p (s n) -> p s n", s=2)
        self.s_all = cut(4, F32, "p (s n) -> p s n", s=2)
        left_over = at[0]
        self.more_raw = cut(RAW_SLOTS * 2, I32, "p (s n) -> p s n", s=RAW_SLOTS)
        self.more_rows = cut(2, F32)
        at[0] = left_over
        self.spare = cut(4, F32, "p (s n) -> p s n", s=2)
        self.spare_halves = [cut(2, F16, "p (b n) -> p b n", b=2) for _ in range(3)]
        self.unit_in = [semaphore(f"unit_in{i}") for i in range(FIRST_SLOTS)]
        self.spread_done = semaphore("spread_done")
        self.centred = semaphore("centred")
        self.scaled = semaphore("scaled")
        self.hi_done = semaphore("hi_done")
        self.lo_done = semaphore("lo_done")
        self.passed = semaphore("unit_passed")

    def slots(self, c):
        return FIRST_SLOTS if isinstance(c, int) and c == 0 else RAW_SLOTS

    def staged(self, c, k):
        i = k % self.slots(c)
        return (self.raw if i < RAW_SLOTS else self.more_raw)[:, i % RAW_SLOTS, :]

    def row(self, c, k, which):
        p = 64 * (k % 2) + 32 * which
        return (self.rows if k % self.slots(c) < RAW_SLOTS else self.more_rows)[p:p + 1, :]

    def wait_loaded(self, eng, c, k):
        first, n = 48 * (UNITS // FIRST_SLOTS), self.slots(c)
        before = 0 if n == FIRST_SLOTS else (c - 1) * (48 * (UNITS // RAW_SLOTS)) + first
        eng.wait_ge(self.unit_in[k % n], before + 48 * (k // n + 1))

    def load(self, sp, c, k):
        n = self.slots(c)
        arrived = self.unit_in[k % n]
        sp.wait_ge(self.lo_done, c * UNITS + k + 1 + FIRST_SLOTS - n)
        hold(sp, self.passed)
        sp.dma_start(self.staged(c, k), self.w_units[c, k]).then_inc(arrived, 16)
        sp.dma_start(self.row(c, k, 0), self.z_units[c, k:k + 1, :].bitcast(F32)).then_inc(arrived, 16)
        sp.dma_start(self.row(c, k, 1), self.s_units[c, k:k + 1, :]).then_inc(arrived, 16)

    def spread(self, pool, c, k):
        self.wait_loaded(pool, c, k)
        pool.wait_ge(self.scaled, c * UNITS + k + 1)
        hold(pool, self.passed)
        self.nc.gpsimd.partition_broadcast(self.z_all[:, k % 2, :], self.row(c, k, 0).bitcast(I32), channels=P).then_inc(self.spread_done, 1)
        self.nc.gpsimd.partition_broadcast(self.s_all[:, k % 2, :], self.row(c, k, 1), channels=P).then_inc(self.spread_done, 1)

    def scale(self, dve, c, k):
        raw = self.staged(c, k)
        w = raw.bitcast(F32)
        dve.wait_ge(self.spread_done, c * (2 * UNITS) + 2 * k + 2)
        self.wait_loaded(dve, c, k)
        self.nc.vector.tensor_tensor(w, raw, self.z_all[:, k % 2, :], ALU.subtract).then_inc(self.centred, 1)
        dve.wait_ge(self.centred, c * UNITS + k + 1)
        self.nc.vector.scalar_tensor_tensor(out=w, in0=w, scalar=W_SCALE, in1=self.s_all[:, k % 2, :], op0=ALU.mult,
                                            op1=ALU.mult).then_inc(self.scaled, 1)

    def high(self, act, c, s, k):
        act.wait_ge(self.scaled, c * UNITS + k + 1 + SCALED_CREDIT)
        self.nc.scalar.activation(self.sets[s][0][:, k, :], self.staged(c, k).bitcast(F32), ACT.Copy).then_inc(self.hi_done, 1)

    def low(self, dve, c, s, k):
        dve.wait_ge(self.hi_done, c * UNITS + k + 1)
        self.nc.vector.tensor_tensor(self.sets[s][1][:, k, :], self.staged(c, k).bitcast(F32), self.sets[s][0][:, k, :],
                                     ALU.subtract).then_inc(self.lo_done, 1)


def attention(nc, xT, x, wqkvT, woT, rotary, const16, const32, x1, shared, units):
    with ExitStack() as ctx:
        sb = lambda name, shape, dt: ctx.enter_context(nc.sbuf_tensor(name, shape, dt))
        sem = lambda name: ctx.enter_context(nc.semaphore(name))

        wqkv = [shared[:, p * KT * QKV:(p + 1) * KT * QKV].rearrange("p (k n) -> p k n", k=KT) for p in range(2)]
        wo = [sb(f"wo{p}", [P, KT, HID], F16) for p in range(2)]
        xs = [sb(f"xs{p}", [P, KT, SEQ], F16) for p in range(2)]
        xin = sb("xin", [P, 4, SEQ], F32)
        q_stack = sb("q_stack", [P, 4, PER_KV, SEQ], F16)
        k_stack = sb("k_stack", [P, KV_HEADS, SEQ], F16)
        stage = sb("stage", [P, 2, 2, SEQ], F16)
        probs = sb("probs", [P, PER_KV, 1280], F32)
        w_in = probs[:, :, :].rearrange("p a b -> p (a b)")
        ot = [sb(f"ot{p}", [P, KV_HEADS, SEQ], F16) for p in range(2)]
        v = sb("v", [P, SEQ_TILES, KV], F32)
        rot = sb("rot", [P, 2, SEQ], F32)
        c16 = sb("c16", [P, 4 * P + SEQ], F16)
        c32 = sb("c32", [P, 3 * N_CHUNKS], F32)
        ones = sb("ones", [P, HD], F32)
        zero = sb("zero", [P, N_CHUNKS], F32)
        r_cos = sb("r_cos", [P, SEQ], F32)
        r_sin = sb("r_sin", [P, SEQ], F32)
        r_out = sb("r_out", [P, SEQ], F32)
        sum_turned = sb("sum_turned", [P, SEQ], F32)
        inv_turned = sb("inv_turned", [P, SEQ // 32], F32)
        row_inv = sb("row_inv", [P, SEQ], F32)
        o_norm = sb("o_norm", [P, SEQ], F32)
        chunk_max = sb("chunk_max", [P, 2, PER_KV, N_CHUNKS], F32)
        left = sb("left", [P, 2, PER_KV, N_CHUNKS], F32)
        top8 = sb("top8", [P, 2, PER_KV, TOP], F32)
        pen = sb("pen", [P, 2, PER_KV, N_CHUNKS], F32)
        pen_edge = sb("pen_edge", [P, 2, PER_KV, BLOCK_CHUNKS], F32)
        edge = sb("edge", [P, 2, PER_KV], F32)
        bias = sb("bias", [P, SEQ_TILES, PER_KV, N_CHUNKS], F16)
        edge_diag = sb("edge_diag", [P, 2, 2, PER_KV, P], F16)
        y = sb("y", [P, 2, HID], F32)
        stats = sb("stats", [P, 2, 2, 6], F32)
        mean_var = sb("mean_var", [P, 2, 2], F32)
        var_eps = sb("var_eps", [P, 2], F32)
        rstd = sb("rstd", [P, 2], F32)
        power = sb("power", [P, 1], F32)

        bank = [ctx.enter_context(nc.psum_tensor(f"bank{i}", [P, 512], F32)) for i in range(8)]
        s_bank, st_bank = bank[0:3], bank[3:5]
        o_bank, sum_bank = bank[6], bank[7]
        bias_t = [st_bank[k][:, :].bitcast(F16) for k in range(2)]

        ident = c16[:, 0:P]
        causal_qk = c16[:, P:2 * P]
        causal_kq = c16[:, 2 * P:3 * P]
        same_chunk = c16[:, 3 * P:4 * P]

        const_in = sem("const_in")
        indicator_in = sem("indicator_in")
        w_loaded = [sem(f"w_loaded{s}") for s in range(W_SLOTS + 2)]
        w_hi = sem("w_hi")
        w_lo = sem("w_lo")
        x_loaded = [sem(f"x_loaded{kt}") for kt in range(KT)]
        x_hi = sem("x_hi")
        x_lo = sem("x_lo")
        proj_done = sem("proj_done")
        proj_read = sem("proj_read")
        sin_done = sem("sin_done")
        rotated = sem("rotated")
        rot_hi = sem("rot_hi")
        o_done = sem("o_done")
        edge_ready = sem("edge_ready")
        stage_full = sem("stage_full")
        stage_sent = [sem(f"stage_sent{s}") for s in range(2)]
        s_done = sem("s_done")
        s_read = sem("s_read")
        bias_done = sem("bias_done")
        edge_done = sem("edge_done")
        bias_turned = sem("bias_turned")
        bias_in_a = sem("bias_in_a")
        bias_in_d = sem("bias_in_d")
        st_done = sem("st_done")
        exp_done = sem("exp_done")
        pv_done = sem("pv_done")
        o_read = sem("o_read")
        ot_done = sem("ot_done")
        y_loaded = [sem(f"y_loaded{s}") for s in range(2)]
        y_stored = [sem(f"y_stored{s}") for s in range(2)]
        y_done = sem("y_done")
        var_done = sem("var_done")
        rstd_done = sem("rstd_done")
        pool_set = sem("pool_set")
        dve_step = sem("dve_step")
        passed = sem("passed")

        def batches(eng, body):
            with eng.Fori(0, BATCH - 1) as b:
                body(b, True)
            body(BATCH - 1, False)

        K0, Q0, Q1, K1, V0, Q2, HEAD = 0, 1, 2, 3, 4, 8, 9
        BODY_QUERIES = KV_HEADS - 3
        PROJ = HEAD + BODY_QUERIES + 2 * SEQ_TILES
        ROPES = 10
        QUERY_ROPE = (1, 2, 4, 5, 6, 7, 8, 9)
        HEAD_ROPE = {K0: 0, Q0: 1, Q1: 2, K1: 3, Q2: 4}

        def body_tiles(b):
            return b * PROJ + HEAD

        def next_head(b):
            return body_tiles(b) + BODY_QUERIES

        FIRST_HEAD = (K0, V0, V0 + 1, V0 + 2, V0 + 3, Q0, Q1, K1, Q2)
        FIRST_BANK = (0, 1, 2, 3, 4, 5, 6, 7, 5)

        def head_bank(i):
            return bank[5] if i < V0 or i % 2 == 1 else bank[3]

        UNITS_SPREAD = {KV_HEADS - 2: (0, 1), KV_HEADS - 1: (2, 3)}
        UNITS_BEFORE = 4

        def output_bank(n, more):
            return bank[(5, 3)[n % 2]] if more else bank[(5, 3, 0, 1)[n % 4]]

        BESIDE_OUTPUT = {0: (0, 1, 2), 2: (3, 4, 5), 3: (6, 7, 8), 5: (9, 10)}

        S_UNITS = [(0, range(4)), (1, range(2)), (1, range(2, 4))] + [(i, range(j, j + 1)) for i in (2, 3) for j in range(4)]
        GROUP_S = len(S_UNITS)
        ROW_UNITS = [sum(1 for i, _ in S_UNITS if i <= row) for row in range(SEQ_TILES)]
        PIECES = (((0, 0),), ((0, 1), (384, 3)), ((0, 2),))
        PIECE_AT, PIECE_N = (0, 512, 1024), (512, 512, 256)
        KEY_AT = (0, 512, 1024, 512 + 384)
        GROUP_ST = PER_KV * len(PIECES)

        def w_place(u):
            if u < 2 * KT - 2:
                s = u % W_SLOTS
                return s, u // W_SLOTS, w_in[:, s * QKV:s * QKV + (QKV if u < KT else HID)]
            return W_SLOTS + u % 2, 0, y[:, u % 2, :]

        def x_tile(kt):
            return xin[:, kt, :] if kt < 4 else y[:, (kt - 4) // 2, (kt % 2) * SEQ:(kt % 2 + 1) * SEQ]

        block = ctx.enter_context(nc.Block())

        @block.sync
        def _(sp):
            def load_x(b):
                sp.wait_ge(x_lo, b * KT + KT)
                hold(sp, passed)
                for kt in range(KT):
                    sp.dma_start(x_tile(kt), xT[b, kt * P:(kt + 1) * P, :]).then_inc(x_loaded[kt], 16)

            def send(b, n, query, keys, first=False):
                s = n % 2
                sp.wait_ge(stage_full, b * ROPES + n + 1)
                hold(sp, passed)
                if keys is None:
                    sp.wait_ge(st_done, b * (KV_HEADS * GROUP_ST) + (query - 3) * GROUP_ST + ST_CREDIT)
                elif not first:
                    sp.wait_ge(st_done, b * (KV_HEADS * GROUP_ST) - (1 - keys) * PER_KV * GROUP_ST + ST_CREDIT)
                for j in range(PER_KV):
                    for row, part in enumerate((0, 1, 0) if keys is None else (0, 0, 1)):
                        to = (q_stack[32 * row:32 * row + 32, query % 4, j, :] if keys is None else
                              k_stack[32 * row:32 * row + 32, PER_KV * keys + j, :])
                        sp.dma_start(to, stage[32 * j:32 * j + 32, s, part, :]).then_inc(stage_sent[s], 16)

            def load_w(u):
                s, use, to = w_place(u)
                if use:
                    sp.wait_ge(w_lo, u - W_SLOTS + 1)
                elif u >= W_SLOTS:
                    sp.wait_ge(x_lo, KT + X_CREDIT)
                kt = u % KT
                src = wqkvT[kt * P:(kt + 1) * P, :] if u < KT else woT[kt * P:(kt + 1) * P, :]
                sp.dma_start(to, src).then_inc(w_loaded[s], 16)

            for kt in range(KT):
                sp.dma_start(x_tile(kt), xT[0, kt * P:(kt + 1) * P, :]).then_inc(x_loaded[kt], 16)
                load_w(kt)
            sp.dma_start(c16[:, :], const16).then_inc(const_in, 16)
            sp.dma_start(c32[:, :], const32).then_inc(const_in, 16)
            sp.dma_start(rot[:, :, :], rotary).then_inc(const_in, 16)
            for kv in range(KV_HEADS):
                sp.dma_start(k_stack[96:128, kv, :], const16[96:128, 4 * P:]).then_inc(indicator_in, 16)
            for kt in range(W_SLOTS):
                load_w(KT + kt)
            send(0, HEAD_ROPE[K0], None, 0, True)
            send(0, HEAD_ROPE[Q0], 0, None)
            for kt in range(W_SLOTS, KT):
                load_w(KT + kt)
            send(0, HEAD_ROPE[Q1], 1, None)
            send(0, HEAD_ROPE[K1], None, 1, True)
            send(0, HEAD_ROPE[Q2], 2, None)
            sp.wait_ge(w_lo, 2 * KT)

            def send_first(b):
                send(b, 0, None, 0)
                send(b, 1, 0, None)
                send(b, 2, 1, None)

            def send_second(b):
                send(b, 3, None, 1)
                send(b, 4, 2, None)

            def batch(b, more):
                for q in range(3, KV_HEADS):
                    send(b, QUERY_ROPE[q], q, None)
                    if more and q == 4:
                        for s in range(2):
                            sp.wait_ge(y_stored[s], b * 32 + 16)
                            hold(sp, passed)
                        load_x(b + 1)
                if more:
                    sp.wait_ge(x_lo, (b + 1) * KT + KT + X_CREDIT)
                    hold(sp, passed)
                for s in range(2):
                    if not more:
                        sp.wait_ge(y_stored[s], b * 32 + 16)
                    sp.dma_start(y[:, s, :], x[b, s * P:(s + 1) * P, :]).then_inc(y_loaded[s], 16)
                if more:
                    send_first(b + 1)
                    send_second(b + 1)
                if not more:
                    sp.wait_ge(proj_done, next_head(b))
                    for k in range(UNITS - 2):
                        units.load(sp, 0, k)
                for t in range(SEQ_TILES):
                    if not more and t == 1:
                        for k in range(UNITS - 2, UNITS):
                            units.load(sp, 0, k)
                    s = t % 2
                    sp.wait_ge(y_done, b * SEQ_TILES + t + 1)
                    hold(sp, passed)
                    sp.dma_start(x1[b, t * P:(t + 1) * P, :], y[:, s, :]).then_inc(y_stored[s], 16)
                    if t + 2 < SEQ_TILES:
                        sp.wait_ge(y_stored[s], b * 32 + 32)
                        hold(sp, passed)
                        sp.dma_start(y[:, s, :], x[b, (t + 2) * P:(t + 3) * P, :]).then_inc(y_loaded[s], 16)

            batches(sp, batch)
            for s in range(2):
                sp.wait_ge(y_stored[s], 16 + BATCH * 32)

        @block.gpsimd
        def _(pool):
            pool.sem_inc(st_done, ST_CREDIT)
            pool.sem_inc(bias_turned, ONE)
            pool.sem_inc(pv_done, ONE)
            pool.sem_inc(ot_done, ONE)
            pool.sem_inc(edge_done, EDGE_CREDIT)
            for s in range(2):
                pool.sem_inc(stage_sent[s], STAGE_COUNT)
                pool.sem_inc(y_stored[s], 16)
            nc.gpsimd.memset(power[:, :], -0.5).then_inc(pool_set, 1)
            nc.gpsimd.memset(ones[:, :], 1.0).then_inc(pool_set, 1)
            nc.gpsimd.memset(zero[:, :], 0.0).then_inc(pool_set, 1)
            nc.gpsimd.memset(bias[:, :, :, :], 0.0).then_inc(pool_set, 1)
            pool.wait_ge(pool_set, 4)
            pool.wait_ge(const_in, 48)

            def rotate(b, n, tile):
                pool.wait_ge(proj_read, tile + 1 + PROJ_READ_CREDIT)
                nc.gpsimd.tensor_tensor(r_sin[:, :], r_sin[:, :], rot[:, 1, :], ALU.mult).then_inc(sin_done, 1)
                pool.wait_ge(sin_done, b * ROPES + n + 1)
                nc.gpsimd.tensor_tensor(r_out[:, :], r_cos[:, :], r_sin[:, :], ALU.add).then_inc(rotated, 1)
                pool.wait_ge(rot_hi, b * ROPES + n + 1)
                nc.gpsimd.tensor_tensor(stage[:, n % 2, 1, :], r_out[:, :], stage[:, n % 2, 0, :], ALU.subtract).then_inc(stage_full, 1)

            def edges(b, g, i):
                pool.wait_ge(edge_ready, b * (2 * KV_HEADS) + 2 * g + i - 1)
                pool.wait_ge(st_done, b * (KV_HEADS * GROUP_ST) + (g - 1) * GROUP_ST + ST_CREDIT)
                nc.gpsimd.tensor_tensor(edge_diag[:, g % 2, i - 2, :, :], ident.unsqueeze(1).broadcast_to([P, PER_KV, P]),
                                        edge[:, i % 2, :].unsqueeze(2).broadcast_to([P, PER_KV, P]), ALU.mult).then_inc(edge_done, 1)

            for i in (K0, Q0, Q1, K1, Q2):
                rotate(0, HEAD_ROPE[i], FIRST_HEAD.index(i))
            for i in (2, 3):
                edges(0, 0, i)

            def batch(b, more):
                def low(g):
                    pool.wait_ge(o_done, b * KV_HEADS + g + 1)
                    nc.gpsimd.tensor_tensor(ot[1][:, g, :], o_norm[:, :], ot[0][:, g, :], ALU.subtract).then_inc(ot_done, 1)

                def spread(ks):
                    for k in ks:
                        units.spread(pool, 0, k)
                    pool.wait_ge(units.spread_done, 2 * ks[-1] + 2)

                def norm_power(t):
                    s = t % 2
                    pool.wait_ge(var_done, b * SEQ_TILES + t + 1)
                    nc.gpsimd.tensor_tensor(rstd[:, s:s + 1], var_eps[:, s:s + 1], power[:, :], ALU.pow).then_inc(rstd_done, 1)

                for g in range(KV_HEADS):
                    if more and g == BODY_QUERIES:
                        for kt in range(1, KT, 2):
                            pool.wait_ge(x_hi, (b + 1) * KT + kt + 1)
                            nc.gpsimd.tensor_tensor(xs[1][:, kt, :], x_tile(kt), xs[0][:, kt, :], ALU.subtract).then_inc(x_lo, 1)
                    if g:
                        low(g - 1)
                    if g + 1 < KV_HEADS:
                        for i in (2, 3):
                            edges(b, g + 1, i)
                    if g < BODY_QUERIES:
                        rotate(b, QUERY_ROPE[g + 3], body_tiles(b) + g)
                    elif more:
                        i = (K0, Q0, Q1)[g - BODY_QUERIES]
                        rotate(b + 1, HEAD_ROPE[i], next_head(b) + i)
                    elif g >= KV_HEADS - 2:
                        pool.wait_ge(edge_done, (b + 1) * (2 * KV_HEADS) + EDGE_CREDIT)
                        pool.wait_ge(ot_done, b * KV_HEADS + g + ONE)
                        spread(UNITS_SPREAD[g])
                low(KV_HEADS - 1)
                if more:
                    rotate(b + 1, HEAD_ROPE[K1], next_head(b) + K1)
                    rotate(b + 1, HEAD_ROPE[Q2], next_head(b) + Q2)
                else:
                    pool.wait_ge(ot_done, b * KV_HEADS + KV_HEADS + ONE)
                    spread((4, 5, 6, 7))
                for t in range(SEQ_TILES):
                    norm_power(t)
                    if not more and t < 2:
                        pool.wait_ge(rstd_done, b * SEQ_TILES + t + 1)
                        spread((8 + 2 * t, 9 + 2 * t))
                    if more and t < 2:
                        edges(b + 1, 0, t + 2)

            batches(pool, batch)

        @block.scalar
        def _(act):
            def split_x(b, tiles=range(KT)):
                for kt in tiles:
                    act.wait_ge(x_loaded[kt], b * 16 + 16)
                    nc.scalar.activation(xs[0][:, kt, :], x_tile(kt), ACT.Copy).then_inc(x_hi, 1)

            act.sem_inc(exp_done, EXP_CREDIT)

            def high_w(u):
                s, use, w32 = w_place(u)
                act.wait_ge(w_loaded[s], 16 * (use + 1))
                nc.scalar.activation((wqkv[0] if u < KT else wo[0])[:, u % KT, :], w32, ACT.Copy, scale=W_SCALE).then_inc(w_hi, 1)

            for kt in range(KT):
                split_x(0, [kt])
                high_w(kt)

            def rotated_hi(b, n):
                act.wait_ge(rotated, b * ROPES + n + 1)
                act.wait_ge(stage_sent[n % 2], b * (ROPES // 2 * STAGE_COUNT) + (n // 2 + 1) * STAGE_COUNT)
                nc.scalar.activation(stage[:, n % 2, 0, :], r_out[:, :], ACT.Copy).then_inc(rot_hi, 1)

            rotated_hi(0, HEAD_ROPE[K0])
            rotated_hi(0, HEAD_ROPE[Q0])
            for kt in range(W_SLOTS):
                high_w(KT + kt)
            rotated_hi(0, HEAD_ROPE[Q1])
            rotated_hi(0, HEAD_ROPE[K1])
            for kt in range(W_SLOTS, KT):
                high_w(KT + kt)
            rotated_hi(0, HEAD_ROPE[Q2])

            def batch(b, more):
                for g in range(KV_HEADS):
                    slot = g % 4
                    act.wait_ge(bias_turned, b * (2 * KV_HEADS) + 2 * g + 1 + ONE)
                    nc.scalar.activation(q_stack[96:128, slot, 0:2, :], bias_t[0][96:128, :].rearrange("p (j n) -> p j n", j=2),
                                         ACT.Copy).then_inc(bias_in_a, 1)
                    act.wait_ge(pv_done, b * KV_HEADS + g + ONE)
                    for j in range(PER_KV):
                        for k in range(len(PIECES)):
                            u = j * len(PIECES) + k
                            act.wait_ge(st_done, b * (KV_HEADS * GROUP_ST) + g * GROUP_ST + u + 1 + ST_CREDIT)
                            nc.scalar.activation(probs[:, j, PIECE_AT[k]:PIECE_AT[k] + PIECE_N[k]], st_bank[u % 2][:, 0:PIECE_N[k]],
                                                 ACT.Exp, scale=float(HD) ** -0.5).then_inc(exp_done, 1)
                        if not more and g == KV_HEADS - 1:
                            for k in ((), (0,), (1,), (2,))[j]:
                                units.high(act, 0, 0, k)
                    if g < BODY_QUERIES:
                        rotated_hi(b, QUERY_ROPE[g + 3])
                    elif more:
                        rotated_hi(b + 1, g - BODY_QUERIES)
                    if more and g == BODY_QUERIES - 1:
                        act.wait_ge(proj_done, next_head(b))
                        split_x(b + 1)
                if more:
                    rotated_hi(b + 1, HEAD_ROPE[K1])
                    rotated_hi(b + 1, HEAD_ROPE[Q2])
                else:
                    for k in range(UNITS_BEFORE - 1, UNITS):
                        units.high(act, 0, 0, k)

            batches(act, batch)

        @block.tensor
        def _(pe):
            def product(out, lhs, rhs, n):
                def one(i):
                    kt, (a, c) = i // 3, PARTS[i % 3]
                    return nc.tensor.matmul(out, lhs(a, kt), rhs(c, kt), start=(i == 0), stop=(i == 3 * KT - 1))
                return [lambda i=i: one(i) for i in range(n)]


            def proj_room(tile, back):
                pe.wait_ge(proj_read, tile - back + 1 + PROJ_READ_CREDIT)

            def column_tile(to, c):
                return product(to[:, :], lambda a, kt: wqkv[a][:, kt, c * P:(c + 1) * P], lambda a, kt: xs[a][:, kt, :], 3 * KT)

            def head_tile(i, to):
                if V0 <= i < V0 + SEQ_TILES:
                    t = i - V0
                    return product(to[:, 0:KV], lambda a, kt: xs[a][:, kt, t * P:(t + 1) * P],
                                   lambda a, kt: wqkv[a][:, kt, HID + KV:QKV], 3 * KT)
                return column_tile(to, {K0: KT, K1: KT + 1, Q0: 0, Q1: 1, Q2: 2}[i])

            def scores(b, g, u):
                i, heads = S_UNITS[u]
                pe.wait_ge(s_read, b * (KV_HEADS * GROUP_S) + g * GROUP_S + u + (S_CREDIT if g == 0 and u == 0 else 1))
                n, out = P * (i + 1), s_bank[(g * GROUP_S + u) % 3]
                for k, j in enumerate(heads):
                    nc.tensor.matmul(out[:, k * n:(k + 1) * n], q_stack[0:96, g % 4, j, P * i:n], k_stack[0:96, g, 0:n],
                                     start=(k == 0), stop=True, skip_group_check=True)
                    last = nc.tensor.matmul(out[:, (k + 1) * n - P:(k + 1) * n], ident, causal_qk, start=False, stop=True,
                                            skip_group_check=True)
                last.then_inc(s_done, 1)

            def begin_scores(b, g):
                for n in ((0, 1) if g == 0 else (QUERY_ROPE[g],)):
                    pe.wait_ge(stage_sent[n % 2], b * (ROPES // 2 * STAGE_COUNT) + (n // 2 + 2) * STAGE_COUNT)

            def run(passes, tile, back, beside=(), every=4, b=None):
                beside = list(beside)
                proj_room(tile, back)
                for k, f in enumerate(passes):
                    last = f()
                    if k == len(passes) - 1:
                        last.then_inc(proj_done, 1)
                    if k % every == every - 1 and beside:
                        scores(b, 0, beside.pop(0))

            tiles = [head_tile(i, bank[to]) for i, to in zip(FIRST_HEAD, FIRST_BANK)]
            for kt in range(KT):
                pe.wait_ge(x_lo, kt + 1 + X_CREDIT)
                pe.wait_ge(w_lo, kt + 1)
                for passes in tiles[:Q2]:
                    for f in passes[3 * kt:3 * kt + 3]:
                        last = f()
                    if kt == KT - 1:
                        last.then_inc(proj_done, 1)
            run(tiles[Q2], Q2, 3)
            pe.wait_ge(const_in, 48)
            pe.wait_ge(indicator_in, 16 * KV_HEADS)
            pe.wait_ge(pool_set, 4)
            begin_scores(0, 0)
            for u in range(GROUP_S):
                scores(0, 0, u)

            def batch(b, more):
                def values(g):
                    calls = []
                    for kb in range(SEQ_TILES):
                        for bank_, lhs in ((o_bank, v[:, kb, HD * g:HD * (g + 1)]), (sum_bank, ones[:, :])):
                            def one(kb=kb, bank_=bank_, lhs=lhs):
                                for j in range(PER_KV):
                                    last = nc.tensor.matmul(bank_[32 * j:32 * j + 32, P * kb:SEQ], lhs,
                                                            probs[:, j, KEY_AT[kb]:KEY_AT[kb] + SEQ - P * kb],
                                                            start=(kb == 0), stop=True, skip_group_check=True)
                                return last
                            calls.append(one)
                    return calls

                def scores_by_key(g, j, k):
                    u = j * len(PIECES) + k
                    pe.wait_ge(exp_done, b * (KV_HEADS * GROUP_ST) + g * GROUP_ST + u - 1 + EXP_CREDIT)
                    out = st_bank[u % 2]
                    for at, kb in PIECES[k]:
                        nc.tensor.matmul(out[:, at:at + SEQ - P * kb], k_stack[:, g, P * kb:P * (kb + 1)],
                                         q_stack[:, g % 4, j, P * kb:SEQ], start=(at == 0), stop=True, skip_group_check=True)
                        last = nc.tensor.matmul(out[:, at:at + P], ident, causal_kq, start=False, stop=True, skip_group_check=True)
                        if kb in (1, 2):
                            last = nc.tensor.matmul(out[:, at + P:at + 2 * P], same_chunk, edge_diag[:, g % 2, kb - 1, j, :],
                                                    start=False, stop=True, skip_group_check=True)
                    last.then_inc(st_done, 1)

                def begin_values(g):
                    pe.wait_ge(exp_done, b * (KV_HEADS * GROUP_ST) + (g + 1) * GROUP_ST + EXP_CREDIT)
                    pe.wait_ge(o_read, b * KV_HEADS + g + ONE)

                for g in range(KV_HEADS):
                    if g < BODY_QUERIES:
                        tile, project = body_tiles(b) + g, column_tile(bank[5], g + 3)
                    elif more:
                        i = (K0, Q0, Q1)[g - BODY_QUERIES]
                        tile, project = next_head(b) + i, head_tile(i, head_bank(i))
                    else:
                        tile, project = None, []
                    value = values(g - 1) if g else []
                    ahead = list(range(GROUP_S)) if g + 1 < KV_HEADS else []

                    def scores_ahead(n):
                        for _ in range(n):
                            if ahead:
                                u = ahead.pop(0)
                                if u == 0:
                                    begin_scores(b, g + 1)
                                scores(b, g + 1, u)

                    scores_ahead(3)
                    pe.wait_ge(bias_done, b * (KV_HEADS * SEQ_TILES) + SEQ_TILES * (g + 1))
                    pe.wait_ge(exp_done, b * (KV_HEADS * GROUP_ST) + g * GROUP_ST + EXP_CREDIT)
                    if g == 0:
                        pe.wait_ge(proj_read, body_tiles(b) + PROJ_READ_CREDIT)
                    for k in range(2):
                        for jj in range(2):
                            for i in range(SEQ_TILES):
                                at = jj * SEQ + i * P
                                last = nc.tensor.transpose(bias_t[k][96:128, at:at + P], bias[:, i, 2 * k + jj, :], ident)
                        last.then_inc(bias_turned, 1)
                    if g == 0:
                        proj_room(tile, 1)
                        for f in project[:3 * KT // 2]:
                            f()
                        project = project[3 * KT // 2:]
                    if value:
                        begin_values(g - 1)
                        for n, f in enumerate(value):
                            last = f()
                            if n == len(value) - 1:
                                last.then_inc(pv_done, 1)
                            if n in (3, 7):
                                scores_ahead(1)
                    pe.wait_ge(bias_in_a, b * KV_HEADS + g + 1)
                    pe.wait_ge(bias_in_d, b * KV_HEADS + g + 1)
                    pe.wait_ge(edge_done, b * (2 * KV_HEADS) + 2 * g + 2 + EDGE_CREDIT)
                    if project and g:
                        proj_room(tile, 1)
                    begin = GROUP_ST // 3 if more and g == BODY_QUERIES else 0
                    each = len(project) // (GROUP_ST - begin)
                    for u in range(GROUP_ST):
                        scores_by_key(g, *divmod(u, len(PIECES)))
                        if begin and u == begin:
                            pe.wait_ge(x_lo, (b + 1) * KT + KT + X_CREDIT)
                        for f in project[each * (u - begin):each * (u - begin + 1)] if u >= begin else ():
                            last = f()
                        if project and u == GROUP_ST - 1:
                            last.then_inc(proj_done, 1)
                        if u % 3 != 2:
                            scores_ahead(1)
                    scores_ahead(GROUP_S)
                outputs = next_head(b) + (HEAD if more else 0)

                def output_passes(n):
                    t, h = divmod(n, 2)
                    return product(output_bank(n, more)[:, :], lambda a, kt: ot[a][:, kt, t * P:(t + 1) * P],
                                   lambda a, kt: wo[a][:, kt, h * 512:(h + 1) * 512], 3 * KT)

                early = []
                pe.wait_ge(w_lo, 2 * KT)
                if not more:
                    early = [output_passes(n) for n in range(3)]
                    proj_room(outputs, 1)
                    pe.wait_ge(ot_done, b * KV_HEADS + KV_HEADS - 1 + ONE)
                    for f in early[0][:3 * KT - 3]:
                        f()
                begin_values(KV_HEADS - 1)
                for f in values(KV_HEADS - 1):
                    last = f()
                last.then_inc(pv_done, 1)
                if not more:
                    for passes in early[1:]:
                        for f in passes[:3 * KT - 3]:
                            f()
                if more:
                    for i in range(K1, HEAD):
                        run(head_tile(i, head_bank(i)), next_head(b) + i, 1 if i == K1 else 2)
                    begin_scores(b + 1, 0)
                pe.wait_ge(ot_done, b * KV_HEADS + KV_HEADS + ONE)
                for passes in early:
                    for f in passes[3 * KT - 3:]:
                        last = f()
                    last.then_inc(proj_done, 1)
                for n in range(len(early), 2 * SEQ_TILES):
                    run(output_passes(n), outputs + n, 2 if more else 4, BESIDE_OUTPUT.get(n, ()) if more else (), 6, b + 1)

            batches(pe, batch)

        @block.vector
        def _(dve):
            def split_x(b, tiles):
                for kt in tiles:
                    dve.wait_ge(x_hi, b * KT + kt + 1)
                    nc.vector.tensor_tensor(xs[1][:, kt, :], x_tile(kt), xs[0][:, kt, :], ALU.subtract).then_inc(x_lo, 1)

            dve.sem_inc(x_lo, X_CREDIT)
            dve.sem_inc(units.lo_done, FIRST_SLOTS)
            dve.sem_inc(units.scaled, SCALED_CREDIT)

            def low_w(u):
                kt, w16, w32 = u % KT, wqkv if u < KT else wo, w_place(u)[2]
                dve.wait_ge(w_hi, u + 1)
                nc.vector.scalar_tensor_tensor(out=w16[1][:, kt, :], in0=w32, scalar=W_SCALE, in1=w16[0][:, kt, :],
                                               op0=ALU.mult, op1=ALU.subtract).then_inc(w_lo, 1)

            dve.sem_inc(proj_read, PROJ_READ_CREDIT)
            dve.sem_inc(s_read, S_CREDIT)
            dve.sem_inc(o_read, ONE)
            for kt in range(KT):
                split_x(0, [kt])
                low_w(kt)
            dve.wait_ge(const_in, 48)
            dve.wait_ge(pool_set, 4)

            steps = [0, 0]

            def step(ins):
                steps[0] += 1
                ins.then_inc(dve_step, 1)
                return steps[0]

            def stepped(number):
                dve.wait_ge(dve_step, steps[1] + number)

            def rotate(b, n, number, from_bank):
                tile = from_bank[:, :]
                dve.wait_ge(proj_done, number + 1)
                if not (isinstance(b, int) and b * ROPES + n == 0):
                    dve.wait_ge(rotated, b * ROPES + n)
                nc.vector.tensor_tensor(r_cos[:, :], tile, rot[:, 0, :], ALU.mult)
                nc.vector.stream_shuffle(out=r_sin[:, :], in_=tile, mask=[(i + HD // 2) % HD for i in range(HD)]).then_inc(proj_read, 1)

            def rows_of(i):
                return i % 2, BLOCK_CHUNKS * (i + 1)

            def reduce_rows(b, g, i):
                s, n = rows_of(i)
                for u in range(GROUP_S):
                    if S_UNITS[u][0] != i:
                        continue
                    heads = S_UNITS[u][1]
                    width = len(heads) * n * CHUNK
                    dve.wait_ge(s_done, b * (KV_HEADS * GROUP_S) + g * GROUP_S + u + 1)
                    nc.vector.tensor_reduce(chunk_max[:, s, heads[0]:heads[-1] + 1, 0:n],
                                            s_bank[(g * GROUP_S + u) % 3][:, 0:width].rearrange("p (h c k) -> p h c k", h=len(heads), k=CHUNK),
                                            AX.X, ALU.max).then_inc(s_read, 1)

            def find_top(b, g, i):
                s, n = rows_of(i)
                dve.wait_ge(s_read, b * (KV_HEADS * GROUP_S) + g * GROUP_S + ROW_UNITS[i] + S_CREDIT)
                hold(dve, passed)
                for j in range(PER_KV):
                    last = nc.vector.max(top8[:, s, j, :], chunk_max[:, s, j, 0:n])
                return step(last)

            def mark_taken(i, top_step):
                s, n = rows_of(i)
                stepped(top_step)
                hold(dve, passed)
                for j in range(PER_KV):
                    last = nc.vector.match_replace(left[:, s, j, 0:n], top8[:, s, j, :], chunk_max[:, s, j, 0:n], TAKEN)
                return step(last)

            def find_penalties(i, taken_step):
                s, n = rows_of(i)
                stepped(taken_step)
                far = c32[:, (i - 2) * N_CHUNKS:(i - 2) * N_CHUNKS + n].unsqueeze(1).broadcast_to([P, PER_KV, n])
                own = c32[:, 2 * N_CHUNKS:2 * N_CHUNKS + BLOCK_CHUNKS].unsqueeze(1).broadcast_to([P, PER_KV, BLOCK_CHUNKS])
                nc.vector.scalar_tensor_tensor(out=pen[:, s, :, 0:n], in0=left[:, s, :, 0:n], scalar=TAKEN_OVER, in1=far,
                                               op0=ALU.is_lt, op1=ALU.mult)
                return step(nc.vector.scalar_tensor_tensor(out=pen_edge[:, s, :, :], in0=left[:, s, :, BLOCK_CHUNKS * (i - 1):BLOCK_CHUNKS * i],
                                                           scalar=TAKEN_OVER, in1=own, op0=ALU.is_lt, op1=ALU.mult))

            def bias_rows(b, g, i, step_before):
                s, n = rows_of(i)
                stepped(step_before)
                if i >= 2:
                    dve.wait_ge(edge_done, b * (2 * KV_HEADS) + 2 * g + i - 1 - 2 + EDGE_CREDIT)
                    nc.vector.tensor_reduce(edge[:, s, :], pen_edge[:, s, :, :], AX.X, ALU.add).then_inc(edge_ready, 1)
                    source = pen[:, s, :, 0:n]
                else:
                    source = zero[:, 0:n].unsqueeze(1).broadcast_to([P, PER_KV, n])
                if i == 0:
                    dve.wait_ge(bias_turned, b * (2 * KV_HEADS) + 2 * g + ONE)
                nc.vector.tensor_tensor(bias[:, i, :, 0:n], source, top8[:, s, :, 0:1].broadcast_to([P, PER_KV, n]),
                                        ALU.subtract).then_inc(bias_done, 1)

            def row_tile(b, g, i):
                reduce_rows(b, g, i)
                last = find_top(b, g, i)
                if i >= 2:
                    last = find_penalties(i, mark_taken(i, last))
                bias_rows(b, g, i, last)

            def normalise(b, g):
                dve.wait_ge(pv_done, b * KV_HEADS + g + 1 + ONE)
                last = step(nc.vector.transpose(sum_turned[:, :], sum_bank[:, :]))
                yield
                stepped(last)
                last = step(nc.vector.reciprocal(inv_turned[:, :], sum_turned[:, ::32]))
                yield
                stepped(last)
                last = step(nc.vector.transpose(row_inv[:, :], inv_turned[:, :].unsqueeze(2).broadcast_to([P, SEQ // 32, 32])))
                yield
                stepped(last)
                dve.wait_ge(ot_done, b * KV_HEADS + g + ONE)
                nc.vector.tensor_tensor(o_norm[:, :], o_bank[:, :], row_inv[:, :], ALU.mult).then_inc(o_read, 1)
                yield
                dve.wait_ge(o_read, b * KV_HEADS + g + 1 + ONE)
                if g == 0:
                    dve.wait_ge(proj_done, body_tiles(b))
                nc.vector.tensor_copy(ot[0][:, g, :], o_norm[:, :]).then_inc(o_done, 1)
                yield

            def take_values(b, t, number, from_bank):
                dve.wait_ge(proj_done, number + 1)
                if t == 0:
                    dve.wait_ge(pv_done, b * KV_HEADS + ONE)
                nc.vector.tensor_copy(v[:, t, :], from_bank[:, 0:KV]).then_inc(proj_read, 1)

            def first_rotate(i):
                rotate(0, HEAD_ROPE[i], FIRST_HEAD.index(i), bank[FIRST_BANK[FIRST_HEAD.index(i)]])

            first_rotate(K0)
            for t in range(SEQ_TILES):
                number = FIRST_HEAD.index(V0 + t)
                take_values(0, t, number, bank[FIRST_BANK[number]])
            first_rotate(Q0)
            for kt in range(W_SLOTS):
                low_w(KT + kt)
            first_rotate(Q1)
            row_tile(0, 0, 0)
            row_tile(0, 0, 1)
            first_rotate(K1)
            row_tile(0, 0, 2)
            row_tile(0, 0, 3)
            first_rotate(Q2)
            for kt in range(W_SLOTS, KT):
                low_w(KT + kt)
            assert steps[0] == DVE_GROUP_STEPS, steps

            def batch(b, more):
                steps[0], steps[1] = 0, b * DVE_STEPS + DVE_GROUP_STEPS
                for g in range(KV_HEADS):
                    ahead = g + 1 < KV_HEADS
                    divide = normalise(b, g - 1) if g else iter(())
                    if ahead:
                        reduce_rows(b, g + 1, 0)
                        top0 = find_top(b, g + 1, 0)
                    dve.wait_ge(bias_turned, b * (2 * KV_HEADS) + 2 * g + 2 + ONE)
                    nc.vector.tensor_copy(q_stack[96:128, g % 4, 2:4, :], bias_t[1][96:128, :].rearrange("p (j n) -> p j n", j=2)).then_inc(bias_in_d, 1)
                    if ahead:
                        reduce_rows(b, g + 1, 1)
                        bias_rows(b, g + 1, 0, top0)
                        top1 = find_top(b, g + 1, 1)
                        if more and g == BODY_QUERIES:
                            split_x(b + 1, range(0, KT, 2))
                        next(divide, None)
                        bias_rows(b, g + 1, 1, top1)
                        next(divide, None)
                        reduce_rows(b, g + 1, 2)
                        next(divide, None)
                        top2 = find_top(b, g + 1, 2)
                        next(divide, None)
                        reduce_rows(b, g + 1, 3)
                        next(divide, None)
                        taken2 = mark_taken(2, top2)
                        top3 = find_top(b, g + 1, 3)
                        penalties2 = find_penalties(2, taken2)
                        taken3 = mark_taken(3, top3)
                        bias_rows(b, g + 1, 2, penalties2)
                        bias_rows(b, g + 1, 3, find_penalties(3, taken3))
                    for _ in divide:
                        pass
                    if g < BODY_QUERIES:
                        rotate(b, QUERY_ROPE[g + 3], body_tiles(b) + g, bank[5])
                    elif more:
                        i = (K0, Q0, Q1)[g - BODY_QUERIES]
                        rotate(b + 1, HEAD_ROPE[i], next_head(b) + i, head_bank(i))
                def make_units(ks):
                    for k in ks:
                        units.scale(dve, 0, k)
                        if k:
                            units.low(dve, 0, 0, k - 1)

                if not more:
                    make_units(range(UNITS_BEFORE))
                for _ in normalise(b, KV_HEADS - 1):
                    pass
                if not more:
                    make_units(range(UNITS_BEFORE, 6))
                if more:
                    rotate(b + 1, HEAD_ROPE[K1], next_head(b) + K1, head_bank(K1))
                    for t in range(SEQ_TILES):
                        take_values(b + 1, t, next_head(b) + V0 + t, head_bank(V0 + t))
                    rotate(b + 1, HEAD_ROPE[Q2], next_head(b) + Q2, head_bank(Q2))
                outputs = next_head(b) + (HEAD if more else 0)

                def add_residual(t):
                    s = t % 2
                    dve.wait_ge(y_loaded[s], b * 32 + 16 * (t // 2 + 1))
                    for h in range(2):
                        n = 2 * t + h
                        half = y[:, s, h * 512:(h + 1) * 512]
                        dve.wait_ge(proj_done, outputs + n + 1)
                        nc.vector.scalar_tensor_tensor(out=half, in0=output_bank(n, more)[:, :], scalar=1.0 / (W_SCALE * W_SCALE), in1=half,
                                                       op0=ALU.mult, op1=ALU.add).then_inc(proj_read, 1)
                        dve.wait_ge(proj_read, outputs + n + 1 + PROJ_READ_CREDIT)
                        last = step(nc.vector.bn_stats(stats[:, s, h, :], half))
                    stepped(last)
                    hold(dve, passed)
                    last = step(nc.vector.bn_aggr(mean_var[:, s, :], stats[:, s, :, :].rearrange("p a b -> p (a b)")))
                    stepped(last)
                    nc.vector.tensor_scalar(var_eps[:, s:s + 1], mean_var[:, s, 1:2], EPS, None, ALU.add).then_inc(var_done, 1)

                def norm(t):
                    s = t % 2
                    dve.wait_ge(rstd_done, b * SEQ_TILES + t + 1)
                    nc.vector.tensor_scalar(y[:, s, :], y[:, s, :], mean_var[:, s, 0:1], rstd[:, s:s + 1], ALU.subtract,
                                            ALU.mult).then_inc(y_done, 1)

                if more:
                    row_tile(b + 1, 0, 0)
                add_residual(0)
                if not more:
                    make_units((6, 7))
                if more:
                    row_tile(b + 1, 0, 1)
                norm(0)
                if more:
                    row_tile(b + 1, 0, 2)
                add_residual(1)
                if not more:
                    make_units((8, 9))
                norm(1)
                if more:
                    row_tile(b + 1, 0, 3)
                for t in range(2, SEQ_TILES):
                    add_residual(t)
                    if not more and t == 2:
                        make_units((10, 11))
                        units.low(dve, 0, 0, UNITS - 1)
                    norm(t)
                assert steps[0] == DVE_STEPS - (0 if more else DVE_GROUP_STEPS), steps

            batches(dve, batch)


DVE_GROUP_STEPS = 4 * 1 + 2 * 2
DVE_STEPS = KV_HEADS * DVE_GROUP_STEPS + KV_HEADS * 3 + SEQ_TILES * 3


def mlp(nc, x1, units, ident32, out):
    with ExitStack() as ctx:
        sb = lambda name, shape, dt: ctx.enter_context(nc.sbuf_tensor(name, shape, dt))
        sem = lambda name: ctx.enter_context(nc.semaphore(name))

        TILES = TOK // P
        TT = TOK // 512
        x1s = [sb(f"x1s{p}", [P, KT, TOK], F16) for p in range(2)]
        acc = sb("acc", [P, TILES, HID], F32)
        units.sets[1] = [sb(f"second_set{p}", [P, UNITS, UW], F16) for p in range(2)]
        silu = units.spare
        hidden = sb("hidden", [P, 2, 512], F32)
        hs = [units.spare_halves[0:2], [units.spare_halves[2], sb("hs11", [P, 2, 512], F16)]]
        ident = sb("ident", [P, P], F32)
        stats = sb("stats2", [P, 4, 2, 6], F32)
        mean_var = sb("mean_var2", [P, 4, 2], F32)
        var_eps = sb("var_eps2", [P, 4], F32)
        rstd = sb("rstd2", [P, 4], F32)
        power = sb("power2", [P, 4], F32)
        shift = sb("shift", [P, 4], F32)
        bank = [ctx.enter_context(nc.psum_tensor(f"mbank{i}", [P, 512], F32)) for i in range(8)]
        gate_bank, up_bank, down_bank = bank[0:4:2], bank[1:4:2], bank[4:8]

        ident_in = sem("ident_in")
        acc_in = [sem(f"acc_in{k}") for k in range(4 + TT - 1)]
        turned = sem("turned")
        turned_hi = sem("turned_hi")
        turned_read = sem("turned_read")
        gu_done = sem("gu_done")
        silu_done = sem("silu_done")
        glu_done = sem("glu_done")
        h_hi = sem("h_hi")
        h_lo = sem("h_lo")
        down_done = sem("down_done")
        acc_done = sem("acc_done")
        stats_done = sem("stats_done")
        var_done = sem("var_done2")
        rstd_done = sem("rstd_done2")
        out_done = sem("out_done")
        shift_done = sem("shift_done")
        stored = sem("stored")
        power_set = sem("power_set")

        DOWN_CREDIT = 33
        TILE_DOWNS = 8
        CHUNK_DOWNS = TT * TILE_DOWNS
        GLUS = 2 * TT
        PAIRS = MLP_CHUNKS // 2
        x1_rows = x1.rearrange("b (t p) h -> p (b t) h", p=P)
        out_rows = out.rearrange("b (t p) h -> p (b t) h", p=P)

        def pairs(eng, body):
            body(0, 0, True)
            body(1, 1, True)
            with eng.Fori(1, PAIRS - 1) as i:
                body(i * 2, 0, True)
                body(i * 2 + 1, 1, True)
            body(MLP_CHUNKS - 2, 0, True)
            body(MLP_CHUNKS - 1, 1, False)

        TURNS = 8
        TURN_AFTER = {("glu", 0): 1, ("down", 0): 2, ("down", 1): 3}
        ORDER = (("glu", 0), ("glu", 1), ("down", 0), ("glu", 2), ("down", 1), ("glu", 3), ("down", 2), ("down", 3))
        BEHIND = {("glu", 0): (0, 1), ("glu", 1): (2, 3), ("down", 0): (4,), ("glu", 2): (5, 6), ("down", 1): (7,),
                  ("glu", 3): (8, 9), ("down", 2): (10,), ("down", 3): (11,)}

        block = ctx.enter_context(nc.Block())

        @block.sync
        def _(sp):
            sp.dma_start(ident[:, :], ident32).then_inc(ident_in, 16)
            for t in range(4):
                sp.dma_start(acc[:, t, :], x1_rows[:, t, :]).then_inc(acc_in[t], 16)
            for k in range(UNITS):
                units.load(sp, 1, k)
                if k in (1, 3, 4):
                    tt = (1, 3, 4).index(k) + 1
                    sp.dma_start(acc[:, 4 * tt:4 * tt + 4, :], x1_rows[:, 4 * tt:4 * tt + 4, :]).then_inc(acc_in[3 + tt], 16)
            with sp.Fori(2, MLP_CHUNKS) as c:
                for k in range(UNITS):
                    units.load(sp, c, k)
            for t in range(TILES):
                sp.wait_ge(out_done, t + 1)
                sp.dma_start(out_rows[:, t, :], acc[:, t, :]).then_inc(stored, 16)
            sp.wait_ge(stored, 16 * TILES)

        @block.gpsimd
        def _(pool):
            pool.sem_inc(down_done, DOWN_CREDIT)
            nc.gpsimd.memset(power[:, :], -0.5).then_inc(power_set, 1)
            with pool.Fori(1, MLP_CHUNKS) as c:
                for k in range(UNITS):
                    units.spread(pool, c, k)
            pool.wait_ge(power_set, 1)
            for t in range(TILES):
                pool.wait_ge(var_done, t + 1)
                if t >= 4:
                    pool.wait_ge(out_done, t - 3)
                s = t % 4
                nc.gpsimd.tensor_tensor(rstd[:, s:s + 1], var_eps[:, s:s + 1], power[:, s:s + 1], ALU.pow).then_inc(rstd_done, 1)

        @block.scalar
        def _(act):
            act.sem_inc(glu_done, 2)

            def unit_high(c, s, k):
                if k == 0:
                    act.wait_ge(down_done, c * CHUNK_DOWNS + 1)
                units.high(act, c, s, k)

            def turn(tt, k):
                t, h = 4 * tt + k // 2, k % 2
                act.wait_ge(turned, tt * TURNS + k + 1)
                nc.scalar.activation(x1s[0][:, 4 * h:4 * h + 4, t * P:(t + 1) * P], down_bank[k % 4][:, :].rearrange("p (k t) -> p k t", k=4),
                                     ACT.Copy, scale=X1_SCALE).then_inc(turned_hi, 1)

            for k in range(TURNS):
                turn(0, k)

            def chunk(c, s, more):
                for kind, tt in ORDER:
                    behind = BEHIND[kind, tt] if more else ()
                    if kind == "glu":
                        for j in range(2):
                            n = 2 * tt + j
                            act.wait_ge(gu_done, c * GLUS + n + 1)
                            act.wait_ge(glu_done, c * GLUS + n + 1)
                            nc.scalar.activation(silu[:, j, :], gate_bank[j][:, :], ACT.Silu, scale=1.0 / (W_SCALE * X1_SCALE)).then_inc(silu_done, 1)
                            act.wait_ge(glu_done, c * GLUS + n + 1 + 2)
                            act.wait_ge(down_done, c * CHUNK_DOWNS + TILE_DOWNS * (tt - 1) + DOWN_CREDIT)
                            nc.scalar.activation(hs[0][tt % 2][:, j, :], hidden[:, j, :], ACT.Copy).then_inc(h_hi, 1)
                            if behind:
                                unit_high(c + 1, 1 - s, behind[j])
                    elif behind:
                        unit_high(c + 1, 1 - s, behind[0])
                    elif not more:
                        for t in range(4 * tt, 4 * tt + 4):
                            act.wait_ge(shift_done, t + 1)
                            nc.scalar.activation(acc[:, t, :], acc[:, t, :], ACT.Identity, bias=shift[:, t % 4:t % 4 + 1],
                                                 scale=rstd[:, t % 4:t % 4 + 1]).then_inc(out_done, 1)
                    if isinstance(c, int) and c == 0 and (kind, tt) in TURN_AFTER:
                        for k in range(TURNS):
                            turn(TURN_AFTER[kind, tt], k)

            pairs(act, chunk)

        @block.tensor
        def _(pe):
            pe.wait_ge(ident_in, 16)

            def turn(tt):
                if tt:
                    pe.wait_ge(acc_in[3 + tt], 16)
                if tt >= 2:
                    pe.wait_ge(acc_done, TILE_DOWNS * (tt - 1) + 4)
                for k in range(TURNS):
                    t, h = 4 * tt + k // 2, k % 2
                    if tt == 0 and h == 0:
                        pe.wait_ge(acc_in[t], 16)
                    if tt * TURNS + k >= 4:
                        pe.wait_ge(turned_read, tt * TURNS + k - 3)
                    for q in range(4):
                        last = nc.tensor.transpose(down_bank[k % 4][:, q * P:(q + 1) * P], acc[:, t, (4 * h + q) * P:(4 * h + q + 1) * P], ident[:, :])
                    last.then_inc(turned, 1)

            turn(0)

            def chunk(c, s, more):
                first = isinstance(c, int) and c == 0
                for kind, tt in ORDER:
                    if kind == "glu":
                        if first:
                            pe.wait_ge(turned_read, (tt + 1) * TURNS)
                        for j in range(2):
                            n = 2 * tt + j
                            if n == 0:
                                pe.wait_ge(units.lo_done, c * UNITS + 8 + FIRST_SLOTS)
                            pe.wait_ge(glu_done, c * GLUS + n + 1)
                            for at, to in ((0, gate_bank), (4, up_bank)):
                                for i in range(3 * KT):
                                    kt, (a, x) = i // 3, PARTS[i % 3]
                                    last = nc.tensor.matmul(to[j][:, :], units.sets[s][a][:, at + kt // 2, (kt % 2) * IC + j * P:(kt % 2) * IC + (j + 1) * P],
                                                            x1s[x][:, kt, 512 * tt:512 * (tt + 1)], start=(i == 0), stop=(i == 3 * KT - 1))
                            last.then_inc(gu_done, 1)
                    else:
                        if tt == 0:
                            pe.wait_ge(units.lo_done, c * UNITS + UNITS + FIRST_SLOTS)
                        if first:
                            pe.wait_ge(turned_read, min(tt + 2, TT) * TURNS)
                        pe.wait_ge(h_lo, c * GLUS + 2 * tt + 2)
                        for m in range(TILE_DOWNS):
                            tl, h = divmod(m, 2)
                            pe.wait_ge(acc_done, c * CHUNK_DOWNS + TILE_DOWNS * tt + m + 1)
                            for i in range(6):
                                j, (a, w) = i // 3, PARTS[i % 3]
                                last = nc.tensor.matmul(down_bank[m % 4][:, :], hs[a][tt % 2][:, j, tl * P:(tl + 1) * P],
                                                        units.sets[s][w][:, 8 + 2 * j + h, :], start=(i == 0), stop=(i == 5))
                            last.then_inc(down_done, 1)
                    if first and (kind, tt) in TURN_AFTER:
                        turn(TURN_AFTER[kind, tt])

            pairs(pe, chunk)

        @block.vector
        def _(dve):
            dve.sem_inc(acc_done, 4)

            def turn(tt, k):
                t, h = 4 * tt + k // 2, k % 2
                dve.wait_ge(turned_hi, tt * TURNS + k + 1)
                nc.vector.scalar_tensor_tensor(out=x1s[1][:, 4 * h:4 * h + 4, t * P:(t + 1) * P],
                                               in0=down_bank[k % 4][:, :].rearrange("p (k t) -> p k t", k=4), scalar=X1_SCALE,
                                               in1=x1s[0][:, 4 * h:4 * h + 4, t * P:(t + 1) * P], op0=ALU.mult,
                                               op1=ALU.subtract).then_inc(turned_read, 1)

            for k in range(TURNS):
                turn(0, k)

            def chunk(c, s, more):
                for kind, tt in ORDER:
                    behind = BEHIND[kind, tt] if more else ()
                    if kind == "glu":
                        for j in range(2):
                            n = 2 * tt + j
                            dve.wait_ge(silu_done, c * GLUS + n + 1)
                            nc.vector.scalar_tensor_tensor(out=hidden[:, j, :], in0=up_bank[j][:, :], scalar=1.0 / (W_SCALE * X1_SCALE),
                                                           in1=silu[:, j, :], op0=ALU.mult, op1=ALU.mult).then_inc(glu_done, 1)
                            if behind:
                                units.scale(dve, c + 1, behind[j])
                            dve.wait_ge(h_hi, c * GLUS + n + 1)
                            nc.vector.tensor_tensor(hs[1][tt % 2][:, j, :], hidden[:, j, :], hs[0][tt % 2][:, j, :],
                                                    ALU.subtract).then_inc(h_lo, 1)
                            if behind:
                                units.low(dve, c + 1, 1 - s, behind[j])
                    else:
                        for m in range(TILE_DOWNS):
                            tl, h = divmod(m, 2)
                            part = acc[:, 4 * tt + tl, 512 * h:512 * (h + 1)]
                            dve.wait_ge(down_done, c * CHUNK_DOWNS + TILE_DOWNS * tt + m + 1 + DOWN_CREDIT)
                            nc.vector.scalar_tensor_tensor(out=part, in0=down_bank[m % 4][:, :], scalar=1.0 / W_SCALE, in1=part,
                                                           op0=ALU.mult, op1=ALU.add).then_inc(acc_done, 1)
                            if not more and h == 1:
                                statistics(c, 4 * tt + tl)
                                if tl:
                                    norm_shift(4 * tt + tl - 1)
                            if behind and m == 2:
                                units.scale(dve, c + 1, behind[0])
                            if behind and m == 5:
                                units.low(dve, c + 1, 1 - s, behind[0])
                        if not more:
                            norm_shift(4 * tt + 3)
                    if isinstance(c, int) and c == 0 and (kind, tt) in TURN_AFTER:
                        for k in range(TURNS):
                            turn(TURN_AFTER[kind, tt], k)

            def statistics(c, t):
                s = t % 4
                dve.wait_ge(acc_done, c * CHUNK_DOWNS + 2 * t + 2 + 4)
                for h in range(2):
                    nc.vector.bn_stats(stats[:, s, h, :], acc[:, t, 512 * h:512 * (h + 1)]).then_inc(stats_done, 1)
                dve.wait_ge(stats_done, 3 * t + 2)
                nc.vector.bn_aggr(mean_var[:, s, :], stats[:, s, :, :].rearrange("p a b -> p (a b)")).then_inc(stats_done, 1)
                dve.wait_ge(stats_done, 3 * t + 3)
                nc.vector.tensor_scalar(var_eps[:, s:s + 1], mean_var[:, s, 1:2], EPS, None, ALU.add).then_inc(var_done, 1)

            def norm_shift(t):
                s = t % 4
                dve.wait_ge(rstd_done, t + 1)
                if t >= 4:
                    dve.wait_ge(out_done, t - 3)
                nc.vector.scalar_tensor_tensor(out=shift[:, s:s + 1], in0=mean_var[:, s, 0:1], scalar=-1.0, in1=rstd[:, s:s + 1],
                                               op0=ALU.mult, op1=ALU.mult).then_inc(shift_done, 1)

            pairs(dve, chunk)


def transformer_layer(nc, d_in, x1, out):
    with ExitStack() as ctx:
        shared = ctx.enter_context(nc.sbuf_tensor("shared", [P, 2 * KT * QKV], F16))
        units = ChunkWeights(nc, shared, lambda name: ctx.enter_context(nc.semaphore(name)), d_in["w_units"], d_in["z_units"],
                             d_in["s_units"])
        attention(nc, d_in["xT"], d_in["x"], d_in["wqkvT"], d_in["woT"], d_in["rotary"], d_in["const16"], d_in["const32"], x1, shared, units)
        mlp(nc, x1, units, d_in["ident32"], out)


_OUT = ((BATCH, SEQ, HID), "float32")


def kernel(**inputs):
    import concourse.bacc as _bacc
    from concourse.bass_utils import run_bass_kernel_spmd as _run

    arr = {k: np.asarray(a) for k, a in inputs.items()}
    x = arr["L0_attn_hidden_states"]
    wqkvT = np.concatenate([arr["L0_attn_wq"], arr["L0_attn_wk"], arr["L0_attn_wv"]], axis=0).T

    def wide(w):
        return w.reshape(4, 2, P, MLP_CHUNKS, IC).transpose(3, 0, 2, 1, 4).reshape(MLP_CHUNKS, 4, P, UW)

    def wide_rows(z):
        return z.reshape(4, 2, MLP_CHUNKS, IC).transpose(2, 0, 1, 3).reshape(MLP_CHUNKS, 4, UW)

    def tall(w):
        return w.reshape(MLP_CHUNKS, 2, P, 2, UW).transpose(0, 1, 3, 2, 4).reshape(MLP_CHUNKS, 4, P, UW)

    def tall_rows(z):
        return z.reshape(MLP_CHUNKS, 4, UW)

    g, u, d = "L0_ffn_gate_", "L0_ffn_up_", "L0_ffn_down_"
    rotary, const16, const32 = host_constants()
    arrays = {
        "x": x,
        "xT": x.transpose(0, 2, 1),
        "wqkvT": wqkvT,
        "woT": arr["L0_attn_wo"].T,
        "w_units": np.concatenate([wide(arr[g + "w"]), wide(arr[u + "w"]), tall(arr[d + "w"])], axis=1),
        "z_units": np.concatenate([wide_rows(arr[g + "z"]), wide_rows(arr[u + "z"]), tall_rows(arr[d + "z"])], axis=1),
        "s_units": np.concatenate([wide_rows(arr[g + "s"]), wide_rows(arr[u + "s"]), tall_rows(arr[d + "s"])], axis=1),
        "rotary": rotary,
        "const16": const16,
        "const32": const32,
        "ident32": np.eye(P, dtype=np.float32),
    }
    arrays = {k: np.ascontiguousarray(a) for k, a in arrays.items()}

    nc = _bacc.Bacc("TRN2", target_bir_lowering=False, num_devices=1)
    d_in = {k: nc.dram_tensor(k, a.shape, mybir.dt.from_np(a.dtype), kind="ExternalInput").ap() for k, a in arrays.items()}
    out = nc.dram_tensor("out", _OUT[0], F32, kind="ExternalOutput").ap()
    x1 = nc.dram_tensor("x1", _OUT[0], F32, kind="Internal").ap()
    transformer_layer(nc, d_in, x1, out)
    r = _run(nc, [arrays], core_ids=[0])
    return r.results[0]["out"]
```
